# Optimizing a Trainium2 kernel written in Bass

```python
import numpy as np
import jax
import jax.numpy as jnp

def _softmax(x, axis=-1):
    return jax.nn.softmax(x, axis=axis)

def _gelu(x):
    return jax.nn.gelu(x, approximate=True)

def _silu(x):
    return jax.nn.silu(x)

def _sigmoid(x):
    return jax.nn.sigmoid(x)

def _layernorm(x, axis=-1, eps=1e-05):
    m = jnp.mean(x, axis=axis, keepdims=True)
    v = jnp.var(x, axis=axis, keepdims=True)
    return (x - m) / jnp.sqrt(v + eps)

def _scatter_add(tgt, idx, src, axis=0):
    return tgt.at[idx].add(src)

def _segment_sum(src, seg, n):
    return jax.ops.segment_sum(src, seg, n)
kernel_name = 'mk_adj_resnorm_d4_adj_r2_2f43be'

def setup_inputs(seed: int=0):
    np.random.seed(seed)
    _w = jnp.asarray

    def _rec_inputs():
        import jax
        import jax.numpy as jnp
        _gk = jax.random.key(seed)
        x = -0.0001538 + 1 * jax.random.normal(jax.random.fold_in(_gk, 1), (128, 128, 384), jnp.float32)
        _a = jax.random.bernoulli(jax.random.fold_in(_gk, 2), 0.125, (128, 128, 128))
        _a = jnp.logical_or(_a, jnp.swapaxes(_a, -1, -2))
        _a = jnp.logical_or(_a, jnp.eye(128, dtype=bool))
        adj = _a
        return (x, adj)
    x, adj = _rec_inputs()

    def _L0_gnn_setup():
        import jax, jax.numpy as jnp
        import numpy as np
        B, S, H = (4, 1024, 384)
        NUM_HEADS = 6
        HEAD_SIZE = H // NUM_HEADS
        NEG = -9000000000000000.0

        def _heads(x):
            b, s, _ = x.shape
            return x.reshape(b, s, NUM_HEADS, HEAD_SIZE).transpose(0, 2, 1, 3)
        key = jax.random.key(seed)
        ks = jax.random.split(key, 10)
        seq_inputs = jax.random.normal(ks[0], (B, S, H), dtype=jnp.float32)
        gm = jax.random.randint(ks[1], (B, S, S), 0, 2) > 0
        graph_mask = gm | jnp.eye(S, dtype=bool)[None]
        sc = 1.0 / np.sqrt(H)
        Wq = jax.random.normal(ks[2], (H, H), dtype=jnp.float32) * sc
        bq = jnp.zeros((H,), dtype=jnp.float32)
        Wk = jax.random.normal(ks[3], (H, H), dtype=jnp.float32) * sc
        bk = jnp.zeros((H,), dtype=jnp.float32)
        Wv = jax.random.normal(ks[4], (H, H), dtype=jnp.float32) * sc
        bv = jnp.zeros((H,), dtype=jnp.float32)
        Wf = jax.random.normal(ks[5], (H, H), dtype=jnp.float32) * sc
        bf = jnp.zeros((H,), dtype=jnp.float32)
        return {'seq_inputs': seq_inputs, 'Wq': Wq, 'bq': bq, 'Wk': Wk, 'bk': bk, 'Wv': Wv, 'bv': bv, 'Wf': Wf, 'bf': bf, 'graph_mask': graph_mask}
    _L0_gnn_all = _L0_gnn_setup()
    _L0_gnn_in = {k: v for k, v in _L0_gnn_all.items() if k in ('Wq', 'bq', 'Wk', 'bk', 'Wv', 'bv', 'Wf', 'bf')}
    del _L0_gnn_all

    def _L1_gnn_setup():
        import jax, jax.numpy as jnp
        import numpy as np
        ATT_HEAD = 12
        IN_DIM = 384
        OUT_DIM = IN_DIM // ATT_HEAD
        LEAKY_ALPHA = 0.2
        B, N = (8, 256)
        key = jax.random.key(seed)
        ks = jax.random.split(key, 8)
        feat_in = jax.random.normal(ks[0], (B, N, IN_DIM), dtype=jnp.float32)
        adj = jax.random.randint(ks[1], (B, N, N), 0, 2) > 0
        lim_W = float(np.sqrt(6.0 / (IN_DIM + OUT_DIM)))
        W = jax.random.uniform(ks[2], (ATT_HEAD, IN_DIM, OUT_DIM), minval=-lim_W, maxval=lim_W, dtype=jnp.float32)
        b = jnp.zeros((OUT_DIM,), dtype=jnp.float32)
        lim_w = float(np.sqrt(6.0 / (OUT_DIM + 1)))
        w_src = jax.random.uniform(ks[3], (ATT_HEAD, OUT_DIM, 1), minval=-lim_w, maxval=lim_w, dtype=jnp.float32)
        w_dst = jax.random.uniform(ks[4], (ATT_HEAD, OUT_DIM, 1), minval=-lim_w, maxval=lim_w, dtype=jnp.float32)
        std_H = float(np.sqrt(2.0 / (IN_DIM + IN_DIM)))
        H_w = jax.random.normal(ks[5], (IN_DIM, IN_DIM), dtype=jnp.float32) * std_H
        H_b = jax.random.normal(ks[6], (IN_DIM,), dtype=jnp.float32) * 0.01
        return {'feat_in': feat_in, 'adj': adj, 'W': W, 'b': b, 'w_src': w_src, 'w_dst': w_dst, 'H_w': H_w, 'H_b': H_b}
    _L1_gnn_all = _L1_gnn_setup()
    _L1_gnn_in = {k: v for k, v in _L1_gnn_all.items() if k in ('W', 'b', 'w_src', 'w_dst', 'H_w', 'H_b')}
    del _L1_gnn_all

    def _L2_gnn_setup():
        import jax, jax.numpy as jnp
        import numpy as np
        B, S, H = (4, 1024, 384)
        NUM_HEADS = 6
        HEAD_SIZE = H // NUM_HEADS
        NEG = -9000000000000000.0

        def _heads(x):
            b, s, _ = x.shape
            return x.reshape(b, s, NUM_HEADS, HEAD_SIZE).transpose(0, 2, 1, 3)
        key = jax.random.key(seed)
        ks = jax.random.split(key, 10)
        seq_inputs = jax.random.normal(ks[0], (B, S, H), dtype=jnp.float32)
        gm = jax.random.randint(ks[1], (B, S, S), 0, 2) > 0
        graph_mask = gm | jnp.eye(S, dtype=bool)[None]
        sc = 1.0 / np.sqrt(H)
        Wq = jax.random.normal(ks[2], (H, H), dtype=jnp.float32) * sc
        bq = jnp.zeros((H,), dtype=jnp.float32)
        Wk = jax.random.normal(ks[3], (H, H), dtype=jnp.float32) * sc
        bk = jnp.zeros((H,), dtype=jnp.float32)
        Wv = jax.random.normal(ks[4], (H, H), dtype=jnp.float32) * sc
        bv = jnp.zeros((H,), dtype=jnp.float32)
        Wf = jax.random.normal(ks[5], (H, H), dtype=jnp.float32) * sc
        bf = jnp.zeros((H,), dtype=jnp.float32)
        return {'seq_inputs': seq_inputs, 'Wq': Wq, 'bq': bq, 'Wk': Wk, 'bk': bk, 'Wv': Wv, 'bv': bv, 'Wf': Wf, 'bf': bf, 'graph_mask': graph_mask}
    _L2_gnn_all = _L2_gnn_setup()
    _L2_gnn_in = {k: v for k, v in _L2_gnn_all.items() if k in ('Wq', 'bq', 'Wk', 'bk', 'Wv', 'bv', 'Wf', 'bf')}
    del _L2_gnn_all

    def _L3_gnn_setup():
        import jax, jax.numpy as jnp
        import numpy as np
        ATT_HEAD = 12
        IN_DIM = 384
        OUT_DIM = IN_DIM // ATT_HEAD
        LEAKY_ALPHA = 0.2
        B, N = (8, 256)
        key = jax.random.key(seed)
        ks = jax.random.split(key, 8)
        feat_in = jax.random.normal(ks[0], (B, N, IN_DIM), dtype=jnp.float32)
        adj = jax.random.randint(ks[1], (B, N, N), 0, 2) > 0
        lim_W = float(np.sqrt(6.0 / (IN_DIM + OUT_DIM)))
        W = jax.random.uniform(ks[2], (ATT_HEAD, IN_DIM, OUT_DIM), minval=-lim_W, maxval=lim_W, dtype=jnp.float32)
        b = jnp.zeros((OUT_DIM,), dtype=jnp.float32)
        lim_w = float(np.sqrt(6.0 / (OUT_DIM + 1)))
        w_src = jax.random.uniform(ks[3], (ATT_HEAD, OUT_DIM, 1), minval=-lim_w, maxval=lim_w, dtype=jnp.float32)
        w_dst = jax.random.uniform(ks[4], (ATT_HEAD, OUT_DIM, 1), minval=-lim_w, maxval=lim_w, dtype=jnp.float32)
        std_H = float(np.sqrt(2.0 / (IN_DIM + IN_DIM)))
        H_w = jax.random.normal(ks[5], (IN_DIM, IN_DIM), dtype=jnp.float32) * std_H
        H_b = jax.random.normal(ks[6], (IN_DIM,), dtype=jnp.float32) * 0.01
        return {'feat_in': feat_in, 'adj': adj, 'W': W, 'b': b, 'w_src': w_src, 'w_dst': w_dst, 'H_w': H_w, 'H_b': H_b}
    _L3_gnn_all = _L3_gnn_setup()
    _L3_gnn_in = {k: v for k, v in _L3_gnn_all.items() if k in ('W', 'b', 'w_src', 'w_dst', 'H_w', 'H_b')}
    del _L3_gnn_all
    return {'x': x, 'adj': adj, 'L0_gnn_Wq': _L0_gnn_in['Wq'], 'L0_gnn_bq': _L0_gnn_in['bq'], 'L0_gnn_Wk': _L0_gnn_in['Wk'], 'L0_gnn_bk': _L0_gnn_in['bk'], 'L0_gnn_Wv': _L0_gnn_in['Wv'], 'L0_gnn_bv': _L0_gnn_in['bv'], 'L0_gnn_Wf': _L0_gnn_in['Wf'], 'L0_gnn_bf': _L0_gnn_in['bf'], 'L1_gnn_W': _L1_gnn_in['W'], 'L1_gnn_b': _L1_gnn_in['b'], 'L1_gnn_w_src': _L1_gnn_in['w_src'], 'L1_gnn_w_dst': _L1_gnn_in['w_dst'], 'L1_gnn_H_w': _L1_gnn_in['H_w'], 'L1_gnn_H_b': _L1_gnn_in['H_b'], 'L2_gnn_Wq': _L2_gnn_in['Wq'], 'L2_gnn_bq': _L2_gnn_in['bq'], 'L2_gnn_Wk': _L2_gnn_in['Wk'], 'L2_gnn_bk': _L2_gnn_in['bk'], 'L2_gnn_Wv': _L2_gnn_in['Wv'], 'L2_gnn_bv': _L2_gnn_in['bv'], 'L2_gnn_Wf': _L2_gnn_in['Wf'], 'L2_gnn_bf': _L2_gnn_in['bf'], 'L3_gnn_W': _L3_gnn_in['W'], 'L3_gnn_b': _L3_gnn_in['b'], 'L3_gnn_w_src': _L3_gnn_in['w_src'], 'L3_gnn_w_dst': _L3_gnn_in['w_dst'], 'L3_gnn_H_w': _L3_gnn_in['H_w'], 'L3_gnn_H_b': _L3_gnn_in['H_b']}

def reference(x, adj, L0_gnn_Wq, L0_gnn_bq, L0_gnn_Wk, L0_gnn_bk, L0_gnn_Wv, L0_gnn_bv, L0_gnn_Wf, L0_gnn_bf, L1_gnn_W, L1_gnn_b, L1_gnn_w_src, L1_gnn_w_dst, L1_gnn_H_w, L1_gnn_H_b, L2_gnn_Wq, L2_gnn_bq, L2_gnn_Wk, L2_gnn_bk, L2_gnn_Wv, L2_gnn_bv, L2_gnn_Wf, L2_gnn_bf, L3_gnn_W, L3_gnn_b, L3_gnn_w_src, L3_gnn_w_dst, L3_gnn_H_w, L3_gnn_H_b):
    import jax
    import jax.numpy as jnp

    def _L0_gnn_ref(seq_inputs, Wq, bq, Wk, bk, Wv, bv, Wf, bf, graph_mask):
        import jax, jax.numpy as jnp
        import numpy as np
        B, S, H = (4, 1024, 384)
        NUM_HEADS = 6
        HEAD_SIZE = H // NUM_HEADS
        NEG = -9000000000000000.0

        def _heads(x):
            b, s, _ = x.shape
            return x.reshape(b, s, NUM_HEADS, HEAD_SIZE).transpose(0, 2, 1, 3)
        q = _heads(seq_inputs @ Wq + bq)
        k = _heads(seq_inputs @ Wk + bk)
        v = _heads(seq_inputs @ Wv + bv)
        scores = jnp.einsum('bhqd,bhkd->bhqk', q, k) / np.sqrt(HEAD_SIZE)
        bias = jnp.where(graph_mask, 0.0, NEG)[:, None]
        probs = jax.nn.softmax(scores + bias, axis=-1)
        ctx = jnp.einsum('bhqk,bhkd->bhqd', probs, v)
        ctx = ctx.transpose(0, 2, 1, 3).reshape(seq_inputs.shape[0], seq_inputs.shape[1], H)
        return ctx @ Wf + bf

    def _L1_gnn_ref(feat_in, adj, W, b, w_src, w_dst, H_w, H_b):
        import jax, jax.numpy as jnp
        import numpy as np
        ATT_HEAD = 12
        IN_DIM = 384
        OUT_DIM = IN_DIM // ATT_HEAD
        LEAKY_ALPHA = 0.2
        B, N = (8, 256)
        h = jnp.einsum('bnd,ade->bane', feat_in, W)
        th = jnp.tanh(h)
        attn_src = jnp.einsum('bane,aeo->bano', th, w_src)
        attn_dst = jnp.einsum('bane,aeo->bano', th, w_dst)
        attn = attn_src + jnp.swapaxes(attn_dst, 2, 3)
        attn = jnp.where(attn >= 0, attn, LEAKY_ALPHA * attn)
        mask = ~adj[:, None, :, :]
        attn = jnp.where(mask, jnp.float32(-999.0), attn)
        attn = jax.nn.softmax(attn, axis=-1)
        feat_out = jnp.einsum('banm,bame->bane', attn, h) + b
        feat_out = jnp.swapaxes(feat_out, 1, 2).reshape(feat_in.shape[0], feat_in.shape[1], -1)
        feat_out = jax.nn.elu(feat_out)
        gate = jax.nn.sigmoid(feat_in @ H_w.T + H_b)
        return gate * feat_out + (1.0 - gate) * feat_in

    def _L2_gnn_ref(seq_inputs, Wq, bq, Wk, bk, Wv, bv, Wf, bf, graph_mask):
        import jax, jax.numpy as jnp
        import numpy as np
        B, S, H = (4, 1024, 384)
        NUM_HEADS = 6
        HEAD_SIZE = H // NUM_HEADS
        NEG = -9000000000000000.0

        def _heads(x):
            b, s, _ = x.shape
            return x.reshape(b, s, NUM_HEADS, HEAD_SIZE).transpose(0, 2, 1, 3)
        q = _heads(seq_inputs @ Wq + bq)
        k = _heads(seq_inputs @ Wk + bk)
        v = _heads(seq_inputs @ Wv + bv)
        scores = jnp.einsum('bhqd,bhkd->bhqk', q, k) / np.sqrt(HEAD_SIZE)
        bias = jnp.where(graph_mask, 0.0, NEG)[:, None]
        probs = jax.nn.softmax(scores + bias, axis=-1)
        ctx = jnp.einsum('bhqk,bhkd->bhqd', probs, v)
        ctx = ctx.transpose(0, 2, 1, 3).reshape(seq_inputs.shape[0], seq_inputs.shape[1], H)
        return ctx @ Wf + bf

    def _L3_gnn_ref(feat_in, adj, W, b, w_src, w_dst, H_w, H_b):
        import jax, jax.numpy as jnp
        import numpy as np
        ATT_HEAD = 12
        IN_DIM = 384
        OUT_DIM = IN_DIM // ATT_HEAD
        LEAKY_ALPHA = 0.2
        B, N = (8, 256)
        h = jnp.einsum('bnd,ade->bane', feat_in, W)
        th = jnp.tanh(h)
        attn_src = jnp.einsum('bane,aeo->bano', th, w_src)
        attn_dst = jnp.einsum('bane,aeo->bano', th, w_dst)
        attn = attn_src + jnp.swapaxes(attn_dst, 2, 3)
        attn = jnp.where(attn >= 0, attn, LEAKY_ALPHA * attn)
        mask = ~adj[:, None, :, :]
        attn = jnp.where(mask, jnp.float32(-999.0), attn)
        attn = jax.nn.softmax(attn, axis=-1)
        feat_out = jnp.einsum('banm,bame->bane', attn, h) + b
        feat_out = jnp.swapaxes(feat_out, 1, 2).reshape(feat_in.shape[0], feat_in.shape[1], -1)
        feat_out = jax.nn.elu(feat_out)
        gate = jax.nn.sigmoid(feat_in @ H_w.T + H_b)
        return gate * feat_out + (1.0 - gate) * feat_in
    x = _layernorm(x + _L0_gnn_ref(x, L0_gnn_Wq, L0_gnn_bq, L0_gnn_Wk, L0_gnn_bk, L0_gnn_Wv, L0_gnn_bv, L0_gnn_Wf, L0_gnn_bf, adj), axis=-1)
    x = _layernorm(x + _L1_gnn_ref(x, adj, L1_gnn_W, L1_gnn_b, L1_gnn_w_src, L1_gnn_w_dst, L1_gnn_H_w, L1_gnn_H_b), axis=-1)
    x = _layernorm(x + _L2_gnn_ref(x, L2_gnn_Wq, L2_gnn_bq, L2_gnn_Wk, L2_gnn_bk, L2_gnn_Wv, L2_gnn_bv, L2_gnn_Wf, L2_gnn_bf, adj), axis=-1)
    x = _layernorm(x + _L3_gnn_ref(x, adj, L3_gnn_W, L3_gnn_b, L3_gnn_w_src, L3_gnn_w_dst, L3_gnn_H_w, L3_gnn_H_b), axis=-1)
    return x

_drawn_inputs = setup_inputs


def setup_inputs(seed=0):
    import zlib

    import numpy as np

    out = dict(_drawn_inputs(seed))
    spreads = {'L0_gnn_bq': (0.0, 0.301),
     'L0_gnn_bk': (0.0, 2.0),
     'L0_gnn_bv': (0.0, 0.1),
     'L0_gnn_bf': (0.0, 0.1),
     'L1_gnn_b': (0.0, 0.1),
     'L2_gnn_bq': (0.0, 0.373),
     'L2_gnn_bk': (0.0, 2.0),
     'L2_gnn_bv': (0.0, 0.1),
     'L2_gnn_bf': (0.0, 0.1),
     'L3_gnn_b': (0.0, 0.308)}
    factors = {'L1_gnn_w_src': 2.867, 'L1_gnn_H_b': 36.103, 'L3_gnn_H_b': 36.849}
    for name, (base, spread) in spreads.items():
        noise = np.random.default_rng([zlib.crc32(name.encode()), seed]).standard_normal(out[name].shape)
        drawn = base * np.exp(spread * noise) if base else spread * noise
        out[name] = jnp.asarray(drawn.astype(out[name].dtype))
    for name, factor in factors.items():
        out[name] = (out[name] * factor).astype(out[name].dtype)
    return out
```

```python
import concourse.bass as bass
from concourse import mybir
from contextlib import ExitStack

NGRAPH = 128


def _consts():
    import numpy as np
    ident = np.eye(128, dtype=np.float32)
    sel = np.zeros((96, 2, 12), np.float32)
    sd = np.zeros((128, 2, 3, 96), np.float32)
    for g in range(3):
        for a in range(12):
            sel[32 * g + a, 0, a] = 1.0
            sel[32 * g + 12 + a, 1, a] = 1.0
            sd[32 * (a % 4):32 * (a % 4) + 32, 0, a // 4, 32 * g + a] = 1.0
            sd[32 * (a % 4):32 * (a % 4) + 32, 1, a // 4, 32 * g + 12 + a] = 1.0
    return {"c_ident": ident, "c_sel": sel, "c_sd": sd.reshape(128, -1)}


def build(nc, N, I, mid, out):
    f32, f32r, bf16, u8 = mybir.dt.float32, mybir.dt.float32r, mybir.dt.bfloat16, mybir.dt.uint8
    ALU, ACT, AX = mybir.AluOpType, mybir.ActivationFunctionType, mybir.AxisListType

    D, KT = 384, 3
    AH, DH = 6, 64
    GH, DG = 12, 32
    NEG = -9000000000000000.0 * 8.0
    EPS = 1e-5
    U = 2 * N
    EDGE = 8

    ctx = ExitStack()
    with ctx:
        def sb(name, shape, dt=f32):
            return ctx.enter_context(nc.sbuf_tensor(name, shape, dt))

        def sem(name):
            return ctx.enter_context(nc.semaphore(name))

        def sems(name, n):
            return [sem(f"{name}{i}") for i in range(n)]

        Z = ctx.enter_context(nc.psum_tensor("Z", [128, GH * 128], f32))
        S = ctx.enter_context(nc.psum_tensor("S", [128, 1024], f32))
        W = [ctx.enter_context(nc.psum_tensor(f"W{i}", [128, 512], f32)) for i in range(3)]

        Wq, Wk = [sb(n, [128, 2, KT, D]) for n in ("Wq", "Wk")]
        Wv, Wf, Wg, Wh = [(sb(n + "h", [128, 2, KT, D], f32r), sb(n + "l", [128, 2, KT, D], f32r))
                          for n in ("Wv", "Wf", "Wg", "Wh")]
        stage = sb("stage", [128, 4, KT, D])
        bq, bk = sb("bq", [128, 2, KT]), sb("bk", [128, 2, KT])
        bv, bf, bg, bh = [sb(n, [128, 2, D]) for n in ("bv", "bf", "bg", "bh")]
        wsrc, wdst = sb("wsrc", [128, 2, KT]), sb("wdst", [128, 2, KT])
        Wsd = sb("Wsd", [128, 2, KT, 96])
        sdmask = sb("sdmask", [128, 2, KT, 96])
        ident = sb("ident", [128, 128])
        identb = sb("identb", [128, 128], bf16)
        selc = sb("selc", [96, 2, GH])
        selb = sb("selb", [96, 2, GH, 128], bf16)
        masked = sb("masked", [128, 1])
        mhalf = sb("mhalf", [128, 1])
        eighth = sb("eighth", [128, AH])
        threes = sb("threes", [128, 1])

        x = sb("x", [128, 2, D])
        adj = sb("adj", [128, 2, 128], u8)
        nota = sb("nota", [128, 2, 128], u8)
        nb = sb("nb", [128, 128], bf16)
        xb = sb("xb", [128, D])
        xT = sb("xT", [128, KT, 128])
        xTh, xTl = sb("xTh", [128, KT, 128], f32r), sb("xTl", [128, KT, 128], f32r)
        qT, kT = sb("qT", [128, KT, 128]), sb("kT", [128, KT, 128])
        va = sb("va", [128, D])
        mT = sb("mT", [128, AH])
        pT = sb("pT", [128, AH, 128])
        ptT = sb("ptT", [128, AH, 128])
        bT, lT, rT = sb("bT", [128, AH]), sb("lT", [128, AH]), sb("rT", [128, AH])
        cTh, cTl = sb("cTh", [128, KT, 128], f32r), sb("cTl", [128, KT, 128], f32r)
        y0 = sb("y0", [128, D])
        y = sb("y", [128, 2, D])
        st, mv, ve, rs = sb("st", [128, 6]), sb("mv", [128, 2]), sb("ve", [128, 1]), sb("rs", [128, 1])
        yTh, yTl = sb("yTh", [128, KT, 128], f32r), sb("yTl", [128, KT, 128], f32r)
        ha = sb("ha", [128, 2, D])
        th = sb("th", [128, D])
        gb = sb("gb", [128, D])
        gt = sb("gt", [128, 2, D])
        thT = sb("thT", [128, KT, 128])
        sd = sb("sd", [96, 128], bf16)
        sr = sb("sr", [96, 128])
        sm = sb("sm", [96, 128], bf16)
        zw = sb("zw", [128, GH, 128])
        sdtmp = zw[:, 0:6, 0:96].rearrange("p (s t) c -> p s t c", s=2)
        L = sb("L", [128, GH, 128])
        mG = sb("mG", [128, GH])
        ptG = sb("ptG", [128, GH, 128])
        lG, rG = sb("lG", [128, GH]), sb("rG", [128, GH])
        oT = sb("oT", [128, KT, 128])
        o, om, oe, oq, od, op, os_ = [sb(n, [128, D]) for n in ("o", "om", "oe", "oq", "od", "op", "os")]
        st2, mv2, ve2, rs2 = sb("st2", [128, 6]), sb("mv2", [128, 2]), sb("ve2", [128, 1]), sb("rs2", [128, 1])
        res = sb("res", [128, 2, D])

        s_const = sem("s_const")
        s_w, s_stage = sems("s_w", 2), sems("s_stage", 2)
        s_split = sems("s_split", 2)
        s_x, s_adj, s_st = sems("s_x", 2), sems("s_adj", 2), sems("s_st", 2)
        s_setup, s_pset = sem("s_setup"), sem("s_pset")
        p_xT, p_q, p_k, p_v, p_s, p_ctx, p_f = (sem("p_" + n) for n in "xT q k v s ctx f".split())
        p_yT, p_h, p_g, p_thT, p_sd, p_av, p_o = (sem("p_" + n) for n in "yT h g thT sd av o".split())
        p_z, p_ptG, p_ptT = sems("p_z", 3), sems("p_ptG", 3), sems("p_ptT", 2)
        a_xT, a_xTh, a_cTh, a_yTh, a_th, a_gt, a_thT, a_oT, a_e = (
            sem("a_" + n) for n in "xT xTh cTh yTh th gt thT oT e".split())
        a_nb, a_nota, a_q, a_k = sem("a_nb"), sem("a_nota"), sem("a_q"), sem("a_k")
        a_w, a_ptG = sems("a_w", 3), sems("a_ptG", 3)
        a_eG, a_eT, a_ptT = sems("a_eG", 6), sems("a_eT", 2), sems("a_ptT", 2)
        d_xTl, d_yTl, d_cTl, d_v, d_mT, d_rT = (sem("d_" + n) for n in "xTl yTl cTl v mT rT".split())
        d_y0, d_st, d_mv, d_ve, d_y = (sem("d_" + n) for n in "y0 st mv ve y".split())
        d_h, d_gb, d_hi, d_r1, d_mid, d_sp1, d_sd = (sem("d_" + n) for n in "h gb hi r1 mid sp1 sd".split())
        d_L, d_pred, d_mG = sems("d_L", 3), sems("d_pred", 3), sems("d_mG", 3)
        d_rG, d_o, d_om, d_oq, d_od, d_os, d_st2, d_mv2, d_ve2, d_res = (
            sem("d_" + n) for n in "rG o om oq od os st2 mv2 ve2 res".split())
        g_xb, g_rs, g_rs2, g_bT, g_op, g_ou = (sem("g_" + n) for n in "xb rs rs2 bT op ou".split())
        g_pn = sems("g_pn", 2)

        B_xT, B_f, B_o, B_q, B_k, B_v, B_yT, B_h, B_g, B_thT, B_sd, B_ctx, B_av = (
            W[0], W[2], W[0], W[1], W[2], W[0], W[1], W[0], W[2], W[1], W[1], W[2], W[1])
        S4 = S[:, :].rearrange("p (b c) -> p b c", b=2)[:, :, 0:384].rearrange("p b (j k) -> p b j k", j=3)
        Z3 = Z[:, :].rearrange("p (a m) -> p a m", m=128)
        t3 = lambda ap: ap[:, 0:D].rearrange("p (t n) -> p t n", t=KT)
        bc = lambda ap, n: ap.unsqueeze(len(ap.shape)).to_broadcast(list(ap.shape) + [n])

        def have(u):
            return not isinstance(u, int) or 0 <= u < U

        def dmas(u, par):
            return 8 * u + 16 - 8 * par

        def run(eng, period):
            def doer(u, par, half):
                def do(lag, stage, *args):
                    if half is not None or have(u - lag):
                        stage(u - lag, (par + lag) % 2, (u - lag) // N if half is None else half, *args)
                return do

            for lo, hi, loop in ((0, EDGE, 0), (EDGE, N, 1), (N, N + EDGE, 0), (N + EDGE, U, 1), (U, U + EDGE, 0)):
                if loop and hi > lo:
                    with eng.Fori(lo, hi - 1, 2) as u:
                        for par in range(2):
                            period(doer(u + par if par else u, par, lo // N))
                else:
                    for u in range(lo, hi):
                        period(doer(u, u % 2, None))

        block = ctx.enter_context(nc.Block())

        @block.sync
        def _(sp):
            for dst, src in ((ident[:, :], I["c_ident"]), (selc[:, :, :], I["c_sel"]),
                             (sdmask[:, :, :, :].rearrange("p a t c -> p (a t c)"), I["c_sd"])):
                sp.dma_start(dst, src).then_inc(s_const, 16)
            for i in range(2):
                A_, G_ = f"L{2 * i}_gnn_", f"L{2 * i + 1}_gnn_"
                for t_, n_ in ((Wq, A_ + "Wq"), (Wk, A_ + "Wk")):
                    sp.dma_start(t_[:, i, :, :], I[n_].rearrange("(t p) n -> p t n", p=128)).then_inc(s_w[i], 16)
                for t_, n_ in ((bv, A_ + "bv"), (bf, A_ + "bf"), (bh, G_ + "H_b")):
                    sp.dma_start(t_[:, i, :], I[n_].partition_broadcast(128)).then_inc(s_w[i], 16)
                sp.dma_start(bg[:, i, 0:DG], I[G_ + "b"].partition_broadcast(128)).then_inc(s_w[i], 16)
                for t_, n_ in ((bq, A_ + "bq"), (bk, A_ + "bk"), (wsrc, G_ + "w_src"), (wdst, G_ + "w_dst")):
                    sp.dma_start(t_[:, i, :], I[n_]).then_inc(s_w[i], 16)
                if i == 1:
                    sp.wait_ge(s_split[0], 4)
                for c, n_ in ((0, A_ + "Wv"), (1, A_ + "Wf"), (3, G_ + "H_wT")):
                    sp.dma_start(stage[:, c, :, :], I[n_].rearrange("(t p) n -> p t n", p=128)).then_inc(s_stage[i], 16)
                for t in range(KT):
                    sp.dma_start(stage[:, 2, t, :].rearrange("p (a e) -> p a e", a=GH),
                                 I[G_ + "W"][:, t * 128:(t + 1) * 128, :].rearrange("a p e -> p a e")).then_inc(s_stage[i], 16)

            LATE = 7

            def load(v, p, h):
                sp.wait_ge(s_const, 16 * 3)
                if have(v - 2):
                    sp.wait_ge(g_xb, v - 1)
                    sp.wait_ge(p_xT, v - 1)
                if h == 1:
                    sp.wait_ge(s_st[p], dmas(v - N, p))
                sp.dma_start(x[:, p, :], I["x"][v, :, :] if h == 0 else mid[v - N, :, :]).then_inc(s_x[p], 16)
                sp.wait_ge(s_const, 16 * 3)
                if have(v - 2):
                    sp.wait_ge(a_nota, v - 1)
                    sp.wait_ge(a_nb, v - 1)
                sp.dma_start(adj[:, p, :], I["adj"][v - h * N, :, :]).then_inc(s_adj[p], 16)

            def store(v, p, h):
                sp.wait_ge(s_const, 16 * 3)
                sp.wait_ge(d_res, v + 1)
                sp.dma_start(mid[v, :, :] if h == 0 else out[v - N, :, :], res[:, p, :]).then_inc(s_st[p], 16)

            def period(do):
                do(0, load)
                do(LATE, store)

            run(sp, period)
            for par in range(2):
                sp.wait_ge(s_st[par], dmas(U - 2 + par, par))

        @block.tensor
        def _(pe):
            mm, tr = nc.tensor.matmul, nc.tensor.transpose
            pe.wait_ge(s_setup, 1)
            pe.wait_ge(s_w[0], 16 * 10)
            pe.wait_ge(s_split[0], 4)

            def split3(ps, xh, xl, w, i):
                for t in range(KT):
                    mm(ps, xh[:, t, :], w[0][:, i, t, :], start=(t == 0), stop=False)
                    mm(ps, xh[:, t, :], w[1][:, i, t, :], start=False, stop=False)
                    last = mm(ps, xl[:, t, :], w[0][:, i, t, :], start=False, stop=(t == KT - 1))
                return last

            def tanh_T(v, p, h):
                pe.wait_ge(a_th, v + 1)
                pe.wait_ge(d_yTl, v + 1)
                for t in range(KT):
                    last = tr(B_thT[:, t * 128:(t + 1) * 128], th[:, t * 128:(t + 1) * 128], ident[:, :])
                last.then_inc(p_thT, 1)

            def v_proj(v, p, h):
                pe.wait_ge(d_xTl, v + 1)
                if isinstance(v, int) and v == N:
                    pe.wait_ge(s_split[1], 4)
                if have(v - 1):
                    pe.wait_ge(a_th, v)
                elif have(v - 3):
                    pe.wait_ge(d_o, v - 2)
                else:
                    pe.wait_ge(d_xTl, v + 1)
                split3(B_v[:, 0:D], xTh, xTl, Wv, h).then_inc(p_v, 1)

            def src_dst(v, p, h):
                pe.wait_ge(a_thT, v + 1)
                for t in range(KT):
                    last = mm(B_sd[0:96, 0:128], Wsd[:, h, t, :], thT[:, t, :], start=(t == 0), stop=(t == KT - 1))
                last.then_inc(p_sd, 1)

            def probs_T(v, p, h, b):
                pe.wait_ge(g_pn[b], v + 1)
                for i in range(3):
                    last = tr(S4[:, b, i, :], pT[:, 3 * b + i, :], ident[:, :])
                last.then_inc(p_ptT[b], 1)

            def x_T(v, p, h):
                pe.wait_ge(s_x[p], dmas(v, p))
                if have(v - 1):
                    pe.wait_ge(d_v, v)
                elif have(v - 2):
                    pe.wait_ge(a_th, v - 1)
                elif have(v - 4):
                    pe.wait_ge(d_o, v - 3)
                for t in range(KT):
                    last = tr(B_xT[:, t * 128:(t + 1) * 128], x[:, p, t * 128:(t + 1) * 128], ident[:, :])
                last.then_inc(p_xT, 1)

            def gat_probs_T(v, p, h, t):
                pe.wait_ge(a_eG[2 * t], v + 1)
                pe.wait_ge(a_eG[2 * t + 1], v + 1)
                for a in range(4 * t, 4 * t + 4):
                    last = tr(Z3[:, a, :], L[:, a, :], ident[:, :])
                last.then_inc(p_ptG[t], 1)

            def context(v, p, h):
                pe.wait_ge(a_ptT[0], v + 1)
                pe.wait_ge(a_ptT[1], v + 1)
                pe.wait_ge(d_v, v + 1)
                if have(v - 1):
                    pe.wait_ge(d_gb, v)
                else:
                    pe.wait_ge(a_k, v + 1)
                for f in range(KT):
                    for b in range(2):
                        a = 2 * f + b
                        last = mm(B_ctx[64 * b:64 * b + 64, f * 128:(f + 1) * 128], va[:, a * DH:(a + 1) * DH],
                                  ptT[:, 3 * b + f, :], start=True, stop=True)
                last.then_inc(p_ctx, 1)

            def logits(v, p, h, t):
                pe.wait_ge(d_sd, v + 1)
                if have(v - 1):
                    pe.wait_ge(a_ptG[t], v)
                mm(Z[:, t * 512:(t + 1) * 512], sd[:, :], selb[:, 0, 4 * t:4 * t + 4, :], start=True, stop=False)
                for a in range(4 * t, 4 * t + 4):
                    last = mm(Z3[:, a, :], selb[:, 1, a, :], sd[:, :], start=False, stop=(a == 4 * t + 3))
                last.then_inc(p_z[t], 1)

            def weighted_T(v, p, h):
                pe.wait_ge(a_ptG[0], v + 1)
                pe.wait_ge(a_ptG[1], v + 1)
                pe.wait_ge(a_ptG[2], v + 1)
                if have(v + 1):
                    pe.wait_ge(d_r1, v + 2)
                elif have(v + 2):
                    pe.wait_ge(a_q, v + 3)
                elif have(v - 1):
                    pe.wait_ge(a_oT, v)
                for t in range(3):
                    for i in range(4):
                        a = 4 * t + i
                        last = mm(B_av[32 * i:32 * i + 32, t * 128:(t + 1) * 128], ha[:, p, a * DG:(a + 1) * DG],
                                  ptG[:, a, :], start=True, stop=True)
                last.then_inc(p_av, 1)

            def out_proj(v, p, h):
                pe.wait_ge(d_cTl, v + 1)
                split3(B_f[:, 0:D], cTh, cTl, Wf, h).then_inc(p_f, 1)

            def o_back(v, p, h):
                pe.wait_ge(a_oT, v + 1)
                if have(v + 3):
                    pe.wait_ge(d_xTl, v + 4)
                elif have(v + 2):
                    pe.wait_ge(d_v, v + 3)
                elif have(v + 1):
                    pe.wait_ge(a_th, v + 2)
                elif have(v - 1):
                    pe.wait_ge(d_o, v)
                for t in range(KT):
                    last = tr(B_o[:, t * 128:(t + 1) * 128], oT[:, t, :], ident[:, :])
                last.then_inc(p_o, 1)

            def q_T(v, p, h):
                pe.wait_ge(a_xT, v + 1)
                if have(v - 3):
                    pe.wait_ge(a_oT, v - 2)
                elif have(v - 2):
                    pe.wait_ge(d_r1, v - 1)
                elif have(v - 1):
                    pe.wait_ge(a_q, v)
                for f in range(KT):
                    for t in range(KT):
                        last = mm(B_q[:, f * 128:(f + 1) * 128], Wq[:, h, t, f * 128:(f + 1) * 128], xT[:, t, :],
                                  start=(t == 0), stop=(t == KT - 1))
                last.then_inc(p_q, 1)

            def k_T(v, p, h):
                if have(v - 1):
                    pe.wait_ge(d_y0, v)
                elif have(v - 2):
                    pe.wait_ge(d_gb, v - 1)
                for f in range(KT):
                    for t in range(KT):
                        last = mm(B_k[:, f * 128:(f + 1) * 128], Wk[:, h, t, f * 128:(f + 1) * 128], xT[:, t, :],
                                  start=(t == 0), stop=(t == KT - 1))
                last.then_inc(p_k, 1)

            def y_T(v, p, h):
                pe.wait_ge(d_y, v + 1)
                if have(v + 1):
                    pe.wait_ge(a_q, v + 2)
                elif have(v - 2):
                    pe.wait_ge(a_oT, v - 1)
                elif have(v - 1):
                    pe.wait_ge(d_r1, v)
                for t in range(KT):
                    last = tr(B_yT[:, t * 128:(t + 1) * 128], y[:, p, t * 128:(t + 1) * 128], ident[:, :])
                last.then_inc(p_yT, 1)

            def scores(v, p, h):
                pe.wait_ge(a_nb, v + 1)
                pe.wait_ge(a_q, v + 1)
                pe.wait_ge(a_k, v + 1)
                for b in range(2):
                    mm(S[:, b * 512:b * 512 + 384], identb[:, :],
                       nb[:, :].unsqueeze(1).to_broadcast([128, 3, 128]), start=True, stop=False)
                for f in range(KT):
                    for b in range(2):
                        last = mm(S[:, b * 512 + f * 128:b * 512 + f * 128 + 128], qT[64 * b:64 * b + 64, f, :],
                                  kT[64 * b:64 * b + 64, f, :], start=False, stop=(f == KT - 1))
                last.then_inc(p_s, 1)

            def h_proj(v, p, h):
                pe.wait_ge(d_yTl, v + 1)
                if have(v - 2):
                    pe.wait_ge(d_o, v - 1)
                elif have(v + 1):
                    pe.wait_ge(d_xTl, v + 2)
                else:
                    pe.wait_ge(d_v, v + 1)
                split3(B_h[:, 0:D], yTh, yTl, Wg, h).then_inc(p_h, 1)

            def gate_proj(v, p, h):
                if have(v + 1):
                    pe.wait_ge(a_k, v + 2)
                else:
                    pe.wait_ge(d_y0, v + 1)
                split3(B_g[:, 0:D], yTh, yTl, Wh, h).then_inc(p_g, 1)

            def period(do):
                do(4, tanh_T)
                do(3, v_proj)
                do(4, src_dst)
                do(3, probs_T, 0)
                do(3, probs_T, 1)
                do(2, x_T)
                do(5, gat_probs_T, 0)
                do(3, context)
                do(4, logits, 2)
                do(4, logits, 1)
                do(5, weighted_T)
                do(3, out_proj)
                do(5, o_back)
                do(2, q_T)
                do(2, k_T)
                do(4, logits, 0)
                do(4, gat_probs_T, 2)
                do(3, y_T)
                do(2, scores)
                do(3, h_proj)
                do(3, gate_proj)
                do(4, gat_probs_T, 1)

            run(pe, period)

        @block.scalar
        def _(act):
            av = nc.scalar.activation

            def k_out(v, p, h):
                act.wait_ge(p_k, v + 1)
                for f in range(KT):
                    last = av(kT[:, f, :], B_k[:, f * 128:(f + 1) * 128], ACT.Identity, bias=bk[:, h, f:f + 1])
                last.then_inc(a_k, 1)

            def fifth(v, p, h, t):
                act.wait_ge(p_z[t], v + 1)
                av(zw[:, 4 * t:4 * t + 4, :], Z3[:, 4 * t:4 * t + 4, :], ACT.Copy, scale=0.2).then_inc(a_w[t], 1)

            def y_T_high(v, p, h):
                act.wait_ge(p_yT, v + 1)
                av(yTh[:, :, :], t3(B_yT), ACT.Copy).then_inc(a_yTh, 1)

            def gat_probs_T_out(v, p, h, t):
                act.wait_ge(p_ptG[t], v + 1)
                av(ptG[:, 4 * t:4 * t + 4, :], Z3[:, 4 * t:4 * t + 4, :], ACT.Copy).then_inc(a_ptG[t], 1)

            def gat_exp(v, p, h, c):
                act.wait_ge(d_mG[c // 2], v + 1)
                if have(v - 1):
                    act.wait_ge(d_rG, v)
                for a in range(2 * c, 2 * c + 2):
                    last = av(L[:, a, :], L[:, a, :], ACT.Exp, bias=mG[:, a:a + 1], accum_out=lG[:, a:a + 1])
                last.then_inc(a_eG[c], 1)

            def att_exp(v, p, h, b):
                act.wait_ge(g_bT, v + 1)
                for s in range(3 * b, 3 * b + 3):
                    last = av(pT[:, s, :], S4[:, b, s % 3, :], ACT.Exp, bias=bT[:, s:s + 1], scale=DH ** -0.5,
                              accum_out=lT[:, s:s + 1])
                last.then_inc(a_eT[b], 1)

            def tanh_h(v, p, h):
                act.wait_ge(d_h, v + 1)
                av(th[:, :], B_h[:, 0:D], ACT.Tanh).then_inc(a_th, 1)

            def tanh_T_out(v, p, h):
                act.wait_ge(p_thT, v + 1)
                av(thT[:, :, :], t3(B_thT), ACT.Copy).then_inc(a_thT, 1)

            def mask_not(v, p, h):
                act.wait_ge(s_adj[p], dmas(v, p))
                av(nota[:, p, :], adj[:, p, :], ACT.Copy, scale=-1.0, bias=1.0).then_inc(a_nota, 1)

            def mask_bias(v, p, h):
                act.wait_ge(s_adj[p], dmas(v, p))
                av(nb[:, :], adj[:, p, :], ACT.Copy, scale=-NEG, bias=NEG).then_inc(a_nb, 1)

            def probs_T_out(v, p, h, b):
                act.wait_ge(p_ptT[b], v + 1)
                av(ptT[:, 3 * b:3 * b + 3, :], S4[:, b, :, :], ACT.Copy).then_inc(a_ptT[b], 1)

            def x_T_out(v, p, h):
                act.wait_ge(p_xT, v + 1)
                av(xT[:, :, :], t3(B_xT), ACT.Copy).then_inc(a_xT, 1)

            def context_high(v, p, h):
                act.wait_ge(p_ctx, v + 1)
                av(cTh[:, :, :], t3(B_ctx), ACT.Copy).then_inc(a_cTh, 1)

            def x_T_high(v, p, h):
                av(xTh[:, :, :], t3(B_xT), ACT.Copy).then_inc(a_xTh, 1)

            def weighted_T_out(v, p, h):
                act.wait_ge(p_av, v + 1)
                av(oT[:, :, :], t3(B_av), ACT.Copy).then_inc(a_oT, 1)

            def gate_tanh(v, p, h):
                act.wait_ge(d_gb, v + 1)
                av(gt[:, p, :], gb[:, :], ACT.Tanh, scale=0.5).then_inc(a_gt, 1)

            def elu_exp(v, p, h):
                act.wait_ge(d_om, v + 1)
                av(oe[:, :], om[:, :], ACT.Exp).then_inc(a_e, 1)

            def q_out(v, p, h):
                act.wait_ge(p_q, v + 1)
                for f in range(KT):
                    last = av(qT[:, f, :], B_q[:, f * 128:(f + 1) * 128], ACT.Identity, bias=bq[:, h, f:f + 1])
                last.then_inc(a_q, 1)

            def period(do):
                do(1, k_out)
                do(3, fifth, 0)
                do(2, y_T_high)
                do(3, gat_probs_T_out, 2)
                do(3, gat_exp, 2)
                do(3, gat_exp, 3)
                do(1, att_exp, 0)
                do(2, tanh_h)
                do(1, att_exp, 1)
                do(2, tanh_T_out)
                do(3, gat_exp, 0)
                do(3, gat_exp, 1)
                do(1, mask_not)
                do(0, mask_bias)
                do(1, probs_T_out, 0)
                do(1, probs_T_out, 1)
                do(0, x_T_out)
                do(3, gat_probs_T_out, 1)
                do(3, gat_probs_T_out, 0)
                do(1, context_high)
                do(2, fifth, 2)
                do(0, x_T_high)
                do(3, weighted_T_out)
                do(2, fifth, 1)
                do(2, gate_tanh)
                do(2, gat_exp, 5)
                do(3, elu_exp)
                do(0, q_out)
                do(2, gat_exp, 4)

            run(act, period)

        @block.vector
        def _(dve):
            vec = nc.vector
            n_set = [0]

            def chained(ins):
                n_set[0] += 1
                ins.then_inc(s_pset, 1)
                dve.wait_ge(s_pset, n_set[0])

            def split_weight(i, c):
                dve.wait_ge(s_stage[i], 16 * 6)
                w = (Wv, Wf, Wg, Wh)[c]
                chained(vec.tensor_copy(w[0][:, i, :, :], stage[:, c, :, :]))
                vec.tensor_tensor(w[1][:, i, :, :], stage[:, c, :, :], w[0][:, i, :, :], ALU.subtract)\
                   .then_inc(s_split[i], 1)

            def head_blocks(i):
                dve.wait_ge(s_w[i], 16 * 10)
                chained(vec.tensor_tensor(sdtmp[:, 0, :, :], sdmask[:, 0, :, :], bc(wsrc[:, i, :], 96), ALU.mult))
                chained(vec.tensor_tensor(sdtmp[:, 1, :, :], sdmask[:, 1, :, :], bc(wdst[:, i, :], 96), ALU.mult))
                chained(vec.tensor_tensor(Wsd[:, i, :, :], sdtmp[:, 0, :, :], sdtmp[:, 1, :, :], ALU.add))
                for c in range(1, GH):
                    chained(vec.tensor_copy(bg[:, i, c * DG:(c + 1) * DG], bg[:, i, 0:DG]))

            def second_half(v, p, h):
                if isinstance(v, int) and v == 1:
                    head_blocks(1)
                if isinstance(v, int) and 2 <= v < 6:
                    split_weight(1, v - 2)

            dve.wait_ge(s_const, 16 * 3)
            vec.tensor_copy(identb[:, :], ident[:, :]).then_inc(s_pset, 1)
            vec.tensor_copy(selb[:, :, :, :], bc(selc[:, :, :], 128)).then_inc(s_pset, 1)
            vec.memset(mhalf[:, :], -0.5).then_inc(s_pset, 1)
            vec.memset(threes[:, :], 3.0).then_inc(s_pset, 1)
            vec.memset(eighth[:, :], DH ** -0.5).then_inc(s_pset, 1)
            vec.memset(masked[:, :], -999.0).then_inc(s_pset, 1)
            n_set[0] = 6
            dve.wait_ge(s_pset, n_set[0])
            head_blocks(0)
            vec.memset(masked[:, :], -999.0).then_inc(s_setup, 1)
            for c in range(4):
                split_weight(0, c)
            dve.wait_ge(s_setup, 1)
            dve.wait_ge(s_split[0], 4)

            def gat_max(v, p, h, t):
                dve.wait_ge(d_pred[t], v + 1)
                vec.tensor_reduce(mG[:, 4 * t:4 * t + 4], L[:, 4 * t:4 * t + 4, :], AX.X, ALU.max, negate=True).then_inc(d_mG[t], 1)

            def att_sum(v, p, h):
                dve.wait_ge(p_f, v + 1)
                dve.wait_ge(g_xb, v + 1)
                vec.tensor_tensor(y0[:, :], B_f[:, 0:D], xb[:, :], ALU.add).then_inc(d_y0, 1)

            def gat_divide(v, p, h):
                dve.wait_ge(p_o, v + 1)
                dve.wait_ge(d_rG, v + 1)
                vec.tensor_tensor(o[:, :].rearrange("p (a e) -> p a e", a=GH), B_o[:, 0:D].rearrange("p (a e) -> p a e", a=GH),
                                bc(rG[:, :], DG), ALU.mult).then_inc(d_o, 1)

            def att_stats(v, p, h):
                dve.wait_ge(d_y0, v + 1)
                vec.bn_stats(st[:, :], y0[:, :]).then_inc(d_st, 1)

            def below_zero(v, p, h):
                dve.wait_ge(d_o, v + 1)
                vec.tensor_scalar(om[:, :], o[:, :], 0.0, None, ALU.min).then_inc(d_om, 1)

            def leaky(v, p, h, t):
                dve.wait_ge(a_w[t], v + 1)
                vec.tensor_tensor(L[:, 4 * t:4 * t + 4, :], Z3[:, 4 * t:4 * t + 4, :], zw[:, 4 * t:4 * t + 4, :],
                                ALU.max).then_inc(d_L[t], 1)

            def att_mean_var(v, p, h):
                dve.wait_ge(s_setup, 1)
                dve.wait_ge(d_st, v + 1)
                vec.bn_aggr(mv[:, :], st[:, :]).then_inc(d_mv, 1)

            def elu(v, p, h):
                dve.wait_ge(a_e, v + 1)
                vec.scalar_tensor_tensor(oq[:, :], o[:, :], 0.0, oe[:, :], ALU.max, ALU.add).then_inc(d_oq, 1)

            def att_var_eps(v, p, h):
                dve.wait_ge(d_mv, v + 1)
                vec.tensor_scalar(ve[:, :], mv[:, 1:2], EPS, None, ALU.add).then_inc(d_ve, 1)

            def gat_var_eps(v, p, h):
                dve.wait_ge(d_mv2, v + 1)
                vec.tensor_scalar(ve2[:, :], mv2[:, 1:2], 4.0 * EPS, None, ALU.add).then_inc(d_ve2, 1)

            def elu_less_y(v, p, h):
                dve.wait_ge(d_oq, v + 1)
                vec.scalar_tensor_tensor(od[:, :], oq[:, :], 1.0, y[:, p, :], ALU.subtract, ALU.subtract).then_inc(d_od, 1)

            def att_norm(v, p, h):
                dve.wait_ge(g_rs, v + 1)
                if have(v - 2):
                    dve.wait_ge(d_od, v - 1)
                vec.tensor_scalar(y[:, p, :], y0[:, :], mv[:, 0:1], rs[:, :], ALU.subtract, ALU.mult).then_inc(d_y, 1)

            def mask(v, p, h, t):
                dve.wait_ge(s_setup, 1)
                dve.wait_ge(a_nota, v + 1)
                dve.wait_ge(d_L[t], v + 1)
                vec.copy_predicated(L[:, 4 * t:4 * t + 4, :], nota[:, p, :].unsqueeze(1).to_broadcast([128, 4, 128]),
                                  masked[:, :].unsqueeze(1).to_broadcast([128, 4, 128])).then_inc(d_pred[t], 1)

            def y_T_low(v, p, h):
                dve.wait_ge(a_yTh, v + 1)
                vec.tensor_tensor(yTl[:, :, :], t3(B_yT), yTh[:, :, :], ALU.subtract).then_inc(d_yTl, 1)

            def att_max(v, p, h):
                dve.wait_ge(p_s, v + 1)
                vec.tensor_reduce(mT[:, :].rearrange("p (b j) -> p b j", b=2), S4, AX.X, ALU.max, negate=True).then_inc(d_mT, 1)

            def h_bias(v, p, h):
                dve.wait_ge(p_h, v + 1)
                vec.tensor_tensor(ha[:, p, :], B_h[:, 0:D], bg[:, h, :], ALU.add).then_inc(d_h, 1)

            def att_reciprocal(v, p, h):
                dve.wait_ge(a_eT[0], v + 1)
                dve.wait_ge(a_eT[1], v + 1)
                vec.reciprocal(rT[:, :], lT[:, :]).then_inc(d_rT, 1)

            def gat_norm(v, p, h):
                dve.wait_ge(g_rs2, v + 1)
                if have(v - 2):
                    dve.wait_ge(s_st[p], dmas(v - 2, p))
                vec.tensor_scalar(res[:, p, :], os_[:, :], mv2[:, 0:1], rs2[:, :], ALU.subtract, ALU.mult).then_inc(d_res, 1)

            def gated_sum(v, p, h):
                dve.wait_ge(g_op, v + 1)
                if have(v - 1):
                    dve.wait_ge(d_res, v)
                vec.scalar_tensor_tensor(os_[:, :], oq[:, :], 4.0, op[:, :], ALU.mult, ALU.add).then_inc(d_os, 1)

            def gate_bias(v, p, h):
                dve.wait_ge(p_g, v + 1)
                if have(v - 1):
                    dve.wait_ge(a_gt, v)
                vec.tensor_tensor(gb[:, :], B_g[:, 0:D], bh[:, h, :], ALU.add).then_inc(d_gb, 1)

            def v_bias(v, p, h):
                dve.wait_ge(p_v, v + 1)
                vec.tensor_tensor(va[:, :], B_v[:, 0:D], bv[:, h, :], ALU.add).then_inc(d_v, 1)

            def src_dst_first(v, p, h):
                dve.wait_ge(p_sd, v + 1)
                vec.tensor_copy(sd[:, :], B_sd[0:96, 0:128]).then_inc(d_hi, 1)

            def src_dst_rest(v, p, h):
                dve.wait_ge(d_hi, v + 1)
                vec.tensor_tensor(sr[:, :], B_sd[0:96, 0:128], sd[:, :], ALU.subtract).then_inc(d_r1, 1)

            def src_dst_second(v, p, h):
                dve.wait_ge(d_r1, v + 1)
                vec.tensor_copy(sd[32:64, :], sr[32:64, :]).then_inc(d_sp1, 1)

            def src_dst_mid(v, p, h):
                vec.tensor_copy(sm[:, :], sr[:, :]).then_inc(d_mid, 1)

            def src_dst_third(v, p, h):
                dve.wait_ge(d_mid, v + 1)
                dve.wait_ge(d_sp1, v + 1)
                vec.tensor_tensor(sd[64:96, :], sr[64:96, :], sm[64:96, :], ALU.subtract).then_inc(d_sd, 1)

            def gat_stats(v, p, h):
                dve.wait_ge(d_os, v + 1)
                vec.bn_stats(st2[:, :], os_[:, :]).then_inc(d_st2, 1)

            def context_low(v, p, h):
                dve.wait_ge(a_cTh, v + 1)
                vec.tensor_tensor(cTl[:, :, :], t3(B_ctx), cTh[:, :, :], ALU.subtract).then_inc(d_cTl, 1)

            def x_T_low(v, p, h):
                dve.wait_ge(a_xTh, v + 1)
                dve.wait_ge(a_xT, v + 1)
                vec.tensor_tensor(xTl[:, :, :], t3(B_xT), xTh[:, :, :], ALU.subtract).then_inc(d_xTl, 1)

            def gat_mean_var(v, p, h):
                dve.wait_ge(s_setup, 1)
                dve.wait_ge(d_st2, v + 1)
                vec.bn_aggr(mv2[:, :], st2[:, :]).then_inc(d_mv2, 1)

            def gat_reciprocal(v, p, h):
                dve.wait_ge(a_eG[0], v + 1)
                dve.wait_ge(a_eG[1], v + 1)
                dve.wait_ge(a_eG[2], v + 1)
                dve.wait_ge(a_eG[3], v + 1)
                vec.reciprocal(rG[:, :], lG[:, :]).then_inc(d_rG, 1)

            def period(do):
                do(0, second_half)
                do(3, gat_max, 2)
                do(2, att_sum)
                do(4, gat_divide)
                do(2, att_stats)
                do(4, below_zero)
                do(3, leaky, 1)
                do(2, att_mean_var)
                do(4, elu)
                do(2, att_var_eps)
                do(5, gat_var_eps)
                do(4, elu_less_y)
                do(2, att_norm)
                do(3, mask, 1)
                do(3, gat_max, 1)
                do(2, y_T_low)
                do(1, att_max)
                do(3, leaky, 0)
                do(2, h_bias)
                do(3, mask, 0)
                do(3, gat_max, 0)
                do(1, att_reciprocal)
                do(5, gat_norm)
                do(4, gated_sum)
                do(2, gate_bias)
                do(1, v_bias)
                do(2, src_dst_first)
                do(2, src_dst_rest)
                do(2, src_dst_second)
                do(2, src_dst_mid)
                do(2, src_dst_third)
                do(4, gat_stats)
                do(1, context_low)
                do(2, leaky, 2)
                do(0, x_T_low)
                do(2, mask, 2)
                do(4, gat_mean_var)
                do(3, gat_reciprocal)

            run(dve, period)

        @block.gpsimd
        def _(pool):
            g = nc.gpsimd
            pool.wait_ge(s_setup, 1)

            def tanh_less_3(v, p, h):
                pool.wait_ge(a_gt, v + 1)
                if have(v - 1):
                    pool.wait_ge(d_os, v)
                g.tensor_tensor(op[:, :], gt[:, p, :], threes[:, :].to_broadcast([128, D]), ALU.subtract).then_inc(g_ou, 1)

            def att_rstd(v, p, h):
                pool.wait_ge(d_ve, v + 1)
                g.tensor_tensor(rs[:, :], ve[:, :], mhalf[:, :], ALU.pow).then_inc(g_rs, 1)

            def gat_rstd(v, p, h):
                pool.wait_ge(d_ve2, v + 1)
                g.tensor_tensor(rs2[:, :], ve2[:, :], mhalf[:, :], ALU.pow).then_inc(g_rs2, 1)

            def att_max_scaled(v, p, h):
                pool.wait_ge(d_mT, v + 1)
                g.tensor_tensor(bT[:, :], mT[:, :], eighth[:, :], ALU.mult).then_inc(g_bT, 1)

            def gate_product(v, p, h):
                pool.wait_ge(d_od, v + 1)
                pool.wait_ge(g_ou, v + 1)
                g.tensor_tensor(op[:, :], op[:, :], od[:, :], ALU.mult).then_inc(g_op, 1)

            def residual(v, p, h):
                pool.wait_ge(s_x[p], dmas(v, p))
                g.tensor_tensor(xb[:, :], x[:, p, :], bf[:, h, :], ALU.add).then_inc(g_xb, 1)

            def att_divide(v, p, h, b):
                pool.wait_ge(d_rT, v + 1)
                g.tensor_tensor(pT[:, 3 * b:3 * b + 3, :], pT[:, 3 * b:3 * b + 3, :], bc(rT[:, 3 * b:3 * b + 3], 128),
                                ALU.mult).then_inc(g_pn[b], 1)

            def period(do):
                do(3, tanh_less_3)
                do(1, att_rstd)
                do(4, gat_rstd)
                do(0, att_max_scaled)
                do(3, gate_product)
                do(0, residual)
                do(0, att_divide, 0)
                do(0, att_divide, 1)

            run(pool, period)


def kernel(**inputs):
    import numpy as np
    import concourse.bacc as bacc
    from concourse.bass_utils import run_bass_kernel_spmd

    N = NGRAPH
    nc = bacc.Bacc("TRN2", target_bir_lowering=False, num_devices=1)
    arrays = {}
    for name, a in inputs.items():
        a = np.asarray(a)
        if name.endswith("H_w"):
            name, a = name + "T", a.T
        if name.endswith(("bq", "bk", "w_src", "w_dst")):
            a = a.reshape(3, 128).T
        arrays["in_" + name] = np.ascontiguousarray(a)
    arrays.update({"in_" + n: a for n, a in _consts().items()})
    aps = {n[3:]: nc.dram_tensor(n, a.shape, mybir.dt.from_np(a.dtype), kind="ExternalInput").ap()
           for n, a in arrays.items()}
    mid = nc.dram_tensor("mid", (N, 128, 384), mybir.dt.float32, kind="Internal").ap()
    out = nc.dram_tensor("out", (N, 128, 384), mybir.dt.float32, kind="ExternalOutput").ap()
    build(nc, N, aps, mid, out)
    r = run_bass_kernel_spmd(nc, [arrays], core_ids=[0])
    return r.results[0]["out"]
```

```python
import concourse.bass as bass
from concourse import mybir
from contextlib import ExitStack

NGRAPH = 128


def _consts():
    import numpy as np
    ident = np.eye(128, dtype=np.float32)
    sel = np.zeros((96, 2, 12), np.float32)
    sd = np.zeros((128, 2, 3, 96), np.float32)
    for g in range(3):
        for a in range(12):
            sel[32 * g + a, 0, a] = 1.0
            sel[32 * g + 12 + a, 1, a] = 1.0
            sd[32 * (a % 4):32 * (a % 4) + 32, 0, a // 4, 32 * g + a] = 1.0
            sd[32 * (a % 4):32 * (a % 4) + 32, 1, a // 4, 32 * g + 12 + a] = 1.0
    return {"c_ident": ident, "c_sel": sel, "c_sd": sd.reshape(128, -1)}


def build(nc, N, I, mid, out):
    f32, f32r, bf16, u8 = mybir.dt.float32, mybir.dt.float32r, mybir.dt.bfloat16, mybir.dt.uint8
    ALU, ACT, AX = mybir.AluOpType, mybir.ActivationFunctionType, mybir.AxisListType

    D, KT = 384, 3
    AH, DH = 6, 64
    GH, DG = 12, 32
    NEG = -9000000000000000.0 * 8.0
    EPS = 1e-5
    U = 2 * N
    EDGE = 8

    ctx = ExitStack()
    with ctx:
        def sb(name, shape, dt=f32):
            return ctx.enter_context(nc.sbuf_tensor(name, shape, dt))

        def sem(name):
            return ctx.enter_context(nc.semaphore(name))

        def sems(name, n):
            return [sem(f"{name}{i}") for i in range(n)]

        Z = ctx.enter_context(nc.psum_tensor("Z", [128, GH * 128], f32))
        S = ctx.enter_context(nc.psum_tensor("S", [128, 1024], f32))
        W = [ctx.enter_context(nc.psum_tensor(f"W{i}", [128, 512], f32)) for i in range(3)]

        Wq, Wk, Wv, Wf, Wg, Wh = [(sb(n + "h", [128, 2, KT, D], f32r), sb(n + "l", [128, 2, KT, D], f32r))
                          for n in ("Wq", "Wk", "Wv", "Wf", "Wg", "Wh")]
        cols = sb("cols", [128, 2, 4, KT])
        bq, bk, wsrc, wdst = (cols[:, :, c, :] for c in range(4))
        rows = sb("rows", [128, 2, KT * D + DG])
        bv, bf, bh = (rows[:, :, c * D:(c + 1) * D] for c in range(3))
        bg = rows[:, :, 3 * D:3 * D + DG]
        Wsd = sb("Wsd", [128, 2, KT, 96])
        ident = sb("ident", [128, 128])
        identb = sb("identb", [128, 128], bf16)
        selc = sb("selc", [96, 2, GH])
        selb = sb("selb", [96, 2, GH, 128], bf16)
        masked = sb("masked", [128, 1])
        mhalf = sb("mhalf", [128, 1])
        eighth = sb("eighth", [128, AH])
        threes = sb("threes", [128, 1])

        x = sb("x", [128, 2, D])
        adj = sb("adj", [128, 2, 128], u8)
        nota = sb("nota", [128, 2, 128], u8)
        nb = sb("nb", [128, 128], bf16)
        xb = sb("xb", [128, D])
        xTh, xTl = sb("xTh", [128, KT, 2, 128], f32r), sb("xTl", [128, KT, 2, 128], f32r)
        qT, kT = sb("qT", [128, KT, 2, 128]), sb("kT", [128, KT, 2, 128])
        va = sb("va", [128, D])
        mT = sb("mT", [128, AH])
        pT = sb("pT", [128, AH, 128])
        ptT = sb("ptT", [128, AH, 128])
        bT, lT, rT = sb("bT", [128, AH]), sb("lT", [128, AH]), sb("rT", [128, AH])
        cTh, cTl = sb("cTh", [128, KT, 128], f32r), sb("cTl", [128, KT, 128], f32r)
        y0 = sb("y0", [128, D])
        y = sb("y", [128, 2, D])
        st, mv, ve, rs = sb("st", [128, 6]), sb("mv", [128, 2]), sb("ve", [128, 1]), sb("rs", [128, 1])
        yTh, yTl = sb("yTh", [128, KT, 128], f32r), sb("yTl", [128, KT, 128], f32r)
        ha = sb("ha", [128, 2, D])
        th = sb("th", [128, D])
        gb = sb("gb", [128, D])
        gt = sb("gt", [128, 2, D])
        thT = sb("thT", [128, KT, 128])
        sd = sb("sd", [96, 128], bf16)
        sr = sb("sr", [96, 128])
        sm = sb("sm", [96, 128], bf16)
        zw = sb("zw", [128, GH, 128])
        L = sb("L", [128, GH, 128])
        mG = sb("mG", [128, GH])
        ptG = sb("ptG", [128, GH, 128])
        lG, rG = sb("lG", [128, GH]), sb("rG", [128, GH])
        flat = lambda ap: ap[:, :, :].rearrange("p a m -> p (a m)")
        sdmask, sdtmp = (flat(b_)[:, 0:2 * KT * 96].rearrange("p (s t c) -> p s t c", s=2, t=KT) for b_ in (pT, ptT))
        slot = [flat(b_)[:, 0:KT * D].rearrange("p (t n) -> p t n", t=KT) for b_ in (zw, L, ptG)]
        oT = sb("oT", [128, KT, 128])
        o, om, oe, oq, od, op, os_ = [sb(n, [128, D]) for n in ("o", "om", "oe", "oq", "od", "op", "os")]
        st2, mv2, ve2, rs2 = sb("st2", [128, 6]), sb("mv2", [128, 2]), sb("ve2", [128, 1]), sb("rs2", [128, 1])
        res = sb("res", [128, 2, D])

        s_const = sem("s_const")
        s_slot = sems("s_slot", 3)
        s_split = sems("s_split", 2)
        s_x, s_adj, s_st = sems("s_x", 2), sems("s_adj", 2), sems("s_st", 2)
        s_setup, s_pset = sem("s_setup"), sem("s_pset")
        p_xT, p_q01, p_k01, p_qk2, p_v, p_s, p_ctx, p_f = (sem("p_" + n) for n in "xT q01 k01 qk2 v s ctx f".split())
        p_yT, p_h, p_g, p_thT, p_sd, p_av, p_o = (sem("p_" + n) for n in "yT h g thT sd av o".split())
        p_z, p_ptG, p_ptT = sems("p_z", 3), sems("p_ptG", 3), sems("p_ptT", 2)
        a_xTh, a_cTh, a_yTh, a_th, a_gt, a_thT, a_oT, a_e = (
            sem("a_" + n) for n in "xTh cTh yTh th gt thT oT e".split())
        a_nb, a_nota = sem("a_nb"), sem("a_nota")
        a_q01, a_k01, a_qk2 = sem("a_q01"), sem("a_k01"), sem("a_qk2")
        a_w, a_ptG = sems("a_w", 3), sems("a_ptG", 3)
        a_eG, a_eT, a_ptT = sems("a_eG", 6), sems("a_eT", 2), sems("a_ptT", 2)
        d_xTl, d_yTl, d_cTl, d_v, d_mT, d_rT = (sem("d_" + n) for n in "xTl yTl cTl v mT rT".split())
        d_y0, d_st, d_mv, d_ve, d_y = (sem("d_" + n) for n in "y0 st mv ve y".split())
        d_h, d_gb, d_hi, d_r1, d_mid, d_sp1, d_sd = (sem("d_" + n) for n in "h gb hi r1 mid sp1 sd".split())
        d_L, d_pred, d_mG = sems("d_L", 3), sems("d_pred", 3), sems("d_mG", 3)
        d_rG, d_o, d_om, d_oq, d_od, d_os, d_st2, d_mv2, d_ve2, d_res = (
            sem("d_" + n) for n in "rG o om oq od os st2 mv2 ve2 res".split())
        g_xb, g_rs, g_rs2, g_bT, g_op, g_ou = (sem("g_" + n) for n in "xb rs rs2 bT op ou".split())
        g_pn = sems("g_pn", 2)

        B_xT, B_f, B_o, B_v = (W[1], W[1]), (W[2], W[0]), (W[2], W[2]), (W[2], W[0])
        B_yT, B_h, B_g, B_thT = (W[2], W[2]), (W[1], W[0]), (W[2], W[1]), (W[1], W[0])
        B_sd, B_ctx, B_av = (W[1], W[0]), (W[0], W[0]), (W[2], W[2])
        B_q01, B_k01, B_qk2 = W[0], W[1], W[1]
        pairs = lambda ap: ap.rearrange("p (e n) -> p e n", e=2)
        S4 = S[:, :].rearrange("p (b c) -> p b c", b=2)[:, :, 0:384].rearrange("p b (j k) -> p b j k", j=3)
        Z3 = Z[:, :].rearrange("p (a m) -> p a m", m=128)
        t3 = lambda ap: ap[:, 0:D].rearrange("p (t n) -> p t n", t=KT)
        bc = lambda ap, n: ap.unsqueeze(len(ap.shape)).to_broadcast(list(ap.shape) + [n])

        def have(u):
            return not isinstance(u, int) or 0 <= u < U

        def dmas(u, par):
            return 8 * u + 16 - 8 * par

        def run(eng, period):
            def doer(u, half):
                def do(lag, stage, *args):
                    if half is not None or have(u - lag):
                        stage(u - lag if lag else u, lag % 2, (u - lag) // N if half is None else half, *args)
                return do

            for lo, hi, loop in ((0, EDGE, 0), (EDGE, N, 1), (N, N + EDGE, 0), (N + EDGE, U, 1), (U, U + EDGE, 0)):
                if loop and hi > lo:
                    with eng.Fori(lo, hi - 1, 2) as u:
                        period(doer(u, lo // N))
                else:
                    for u in range(lo, hi, 2):
                        period(doer(u, None))

        block = ctx.enter_context(nc.Block())

        @block.sync
        def _(sp):
            for dst, src in ((ident[:, :], I["c_ident"]), (selc[:, :, :], I["c_sel"]),
                             (flat(pT)[:, 0:2 * KT * 96], I["c_sd"]),
                             (cols[:, :, :, :].rearrange("p i c t -> p (i c t)"), I["cols"]),
                             (rows[:, :, :].rearrange("p i n -> p (i n)"), I["rows"].partition_broadcast(128))):
                sp.dma_start(dst, src).then_inc(s_const, 16)

            def weight(c):
                i, n = c // 6, c % 6
                A_, G_ = f"L{2 * i}_gnn_", f"L{2 * i + 1}_gnn_"
                w = (A_ + "Wq", A_ + "Wk", A_ + "Wv", A_ + "Wf", G_ + "W", G_ + "H_w")[n]
                if c >= 3:
                    sp.wait_ge(s_split[(c - 3) // 6], (c - 3) % 6 + 1)
                sp.dma_start(slot[c % 3], I[w].rearrange("(t p) n -> p t n", p=128)).then_inc(s_slot[c % 3], 16)

            LATE = 6

            def load(v, p, h):
                sp.wait_ge(s_const, 16 * 5)
                if have(v - 2):
                    sp.wait_ge(g_xb, v - 1)
                    sp.wait_ge(p_xT, v - 1)
                if h == 1:
                    sp.wait_ge(s_st[p], dmas(v - N, p))
                sp.dma_start(x[:, p, :], I["x"][v, :, :] if h == 0 else mid[v - N, :, :]).then_inc(s_x[p], 16)
                sp.wait_ge(s_const, 16 * 5)
                if have(v - 2):
                    sp.wait_ge(a_nota, v - 1)
                    sp.wait_ge(a_nb, v - 1)
                sp.dma_start(adj[:, p, :], I["adj"][v - h * N, :, :]).then_inc(s_adj[p], 16)

            def store(v, p, h):
                sp.wait_ge(s_const, 16 * 5)
                sp.wait_ge(d_res, v + 1)
                sp.dma_start(mid[v, :, :] if h == 0 else out[v - N, :, :], res[:, p, :]).then_inc(s_st[p], 16)

            def weights(v, p, h):
                if isinstance(v, int) and v == 0:
                    for c in range(12):
                        weight(c)

            def period(do):
                do(0, load)
                do(LATE, store)
                do(-1, load)
                do(0, weights)
                do(LATE - 1, store)

            run(sp, period)
            for par in range(2):
                sp.wait_ge(s_st[par], dmas(U - 2 + par, par))

        @block.tensor
        def _(pe):
            mm, tr = nc.tensor.matmul, nc.tensor.transpose
            pe.wait_ge(s_setup, 1)

            def pair_T(ps, w, i, f):
                for t in range(KT):
                    wh, wl = (w[c][:, i, t, f * 128:(f + 1) * 128] for c in range(2))
                    mm(ps, wh, xTh[:, t, :, :], start=(t == 0), stop=False)
                    mm(ps, wh, xTl[:, t, :, :], start=False, stop=False)
                    last = mm(ps, wl, xTh[:, t, :, :], start=False, stop=(t == KT - 1))
                return last

            def split3(ps, xh, xl, w, i):
                for t in range(KT):
                    mm(ps, xh[:, t, :], w[0][:, i, t, :], start=(t == 0), stop=False)
                    mm(ps, xh[:, t, :], w[1][:, i, t, :], start=False, stop=False)
                    last = mm(ps, xl[:, t, :], w[0][:, i, t, :], start=False, stop=(t == KT - 1))
                return last

            def y_T(v, p, h):
                pe.wait_ge(d_y, v + 1)
                if p == 0:
                    pe.wait_ge(d_y0, v + 1)
                else:
                    if have(v - 2):
                        pe.wait_ge(d_o, v - 1)
                    else:
                        pe.wait_ge(d_gb, v)
                for t in range(KT):
                    last = tr(B_yT[p][:, t * 128:(t + 1) * 128], y[:, p, t * 128:(t + 1) * 128], ident[:, :])
                last.then_inc(p_yT, 1)

            def probs_T(v, p, h, b):
                pe.wait_ge(g_pn[b], v + 1)
                for i in range(3):
                    last = tr(S4[:, b, i, :], pT[:, 3 * b + i, :], ident[:, :])
                last.then_inc(p_ptT[b], 1)

            def logits(v, p, h, t):
                pe.wait_ge(d_sd, v + 1)
                if have(v - 1):
                    pe.wait_ge(a_ptG[t], v)
                mm(Z[:, t * 512:(t + 1) * 512], sd[:, :], selb[:, 0, 4 * t:4 * t + 4, :], start=True, stop=False)
                for a in range(4 * t, 4 * t + 4):
                    last = mm(Z3[:, a, :], selb[:, 1, a, :], sd[:, :], start=False, stop=(a == 4 * t + 3))
                last.then_inc(p_z[t], 1)

            def h_proj(v, p, h):
                pe.wait_ge(d_yTl, v + 1)
                if isinstance(v, int) and v in (0, N):
                    pe.wait_ge(s_split[v // N], 5)
                if p == 0:
                    if have(v - 1):
                        pe.wait_ge(d_gb, v)
                    elif have(v + 2):
                        pe.wait_ge(d_xTl, v + 3)
                    else:
                        pe.wait_ge(a_k01, v + 1)
                else:
                    if have(v + 1):
                        pe.wait_ge(a_q01, v + 2)
                    else:
                        pe.wait_ge(d_y0, v + 1)
                split3(B_h[p][:, 0:D], yTh, yTl, Wg, h).then_inc(p_h, 1)

            def gate_proj(v, p, h):
                if isinstance(v, int) and v in (0, N):
                    pe.wait_ge(s_split[v // N], 6)
                if p == 0:
                    pe.wait_ge(d_yTl, v + 1)
                else:
                    if have(v + 3):
                        pe.wait_ge(d_xTl, v + 4)
                    elif have(v + 1):
                        pe.wait_ge(a_k01, v + 2)
                    else:
                        pe.wait_ge(d_r1, v)
                split3(B_g[p][:, 0:D], yTh, yTl, Wh, h).then_inc(p_g, 1)

            def tanh_T(v, p, h):
                pe.wait_ge(a_th, v + 1)
                for t in range(KT):
                    last = tr(B_thT[p][:, t * 128:(t + 1) * 128], th[:, t * 128:(t + 1) * 128], ident[:, :])
                last.then_inc(p_thT, 1)

            def gat_probs_T(v, p, h, t):
                pe.wait_ge(a_eG[2 * t], v + 1)
                pe.wait_ge(a_eG[2 * t + 1], v + 1)
                for a in range(4 * t, 4 * t + 4):
                    last = tr(Z3[:, a, :], L[:, a, :], ident[:, :])
                last.then_inc(p_ptG[t], 1)

            def src_dst(v, p, h):
                pe.wait_ge(a_thT, v + 1)
                for t in range(KT):
                    last = mm(B_sd[p][0:96, 0:128], Wsd[:, h, t, :], thT[:, t, :], start=(t == 0), stop=(t == KT - 1))
                last.then_inc(p_sd, 1)

            def context(v, p, h):
                pe.wait_ge(a_ptT[0], v + 1)
                pe.wait_ge(a_ptT[1], v + 1)
                pe.wait_ge(d_v, v + 1)
                if p == 0:
                    if have(v - 1):
                        pe.wait_ge(d_r1, v)
                    else:
                        pe.wait_ge(a_q01, v + 1)
                else:
                    pe.wait_ge(d_v, v + 1)
                for f in range(KT):
                    for b in range(2):
                        a = 2 * f + b
                        last = mm(B_ctx[p][64 * b:64 * b + 64, f * 128:(f + 1) * 128], va[:, a * DH:(a + 1) * DH],
                                  ptT[:, 3 * b + f, :], start=True, stop=True)
                last.then_inc(p_ctx, 1)

            def x_T(v, p, h):
                pe.wait_ge(s_x[p], dmas(v, p))
                if p == 0:
                    if have(v - 2):
                        pe.wait_ge(a_k01, v - 1)
                    elif have(v - 4):
                        pe.wait_ge(d_r1, v - 3)
                    elif have(v - 5):
                        pe.wait_ge(d_gb, v - 4)
                else:
                    if have(v - 3):
                        pe.wait_ge(d_r1, v - 2)
                    elif have(v - 4):
                        pe.wait_ge(d_gb, v - 3)
                    else:
                        pe.wait_ge(d_xTl, v)
                for t in range(KT):
                    last = tr(B_xT[p][:, t * 128:(t + 1) * 128], x[:, p, t * 128:(t + 1) * 128], ident[:, :])
                last.then_inc(p_xT, 1)

            def weighted_T(v, p, h):
                pe.wait_ge(a_ptG[0], v + 1)
                pe.wait_ge(a_ptG[1], v + 1)
                pe.wait_ge(a_ptG[2], v + 1)
                if p == 0:
                    if have(v + 2):
                        pe.wait_ge(d_v, v + 3)
                    else:
                        pe.wait_ge(d_yTl, v + 2)
                else:
                    if have(v + 1):
                        pe.wait_ge(d_gb, v + 2)
                    else:
                        pe.wait_ge(d_o, v)
                for t in range(3):
                    for i in range(4):
                        a = 4 * t + i
                        last = mm(B_av[p][32 * i:32 * i + 32, t * 128:(t + 1) * 128], ha[:, p, a * DG:(a + 1) * DG],
                                  ptG[:, a, :], start=True, stop=True)
                last.then_inc(p_av, 1)

            def out_proj(v, p, h):
                pe.wait_ge(d_cTl, v + 1)
                if isinstance(v, int) and v in (0, N):
                    pe.wait_ge(s_split[v // N], 4)
                if p == 0:
                    if have(v - 2):
                        pe.wait_ge(d_o, v - 1)
                    else:
                        pe.wait_ge(d_v, v + 1)
                else:
                    pe.wait_ge(d_cTl, v + 1)
                split3(B_f[p][:, 0:D], cTh, cTl, Wf, h).then_inc(p_f, 1)

            def o_back(v, p, h):
                pe.wait_ge(a_oT, v + 1)
                for t in range(KT):
                    last = tr(B_o[p][:, t * 128:(t + 1) * 128], oT[:, t, :], ident[:, :])
                last.then_inc(p_o, 1)

            def qk_T_2(v, p, h):
                pe.wait_ge(d_xTl, v + 2)
                if isinstance(v, int) and v in (0, N):
                    pe.wait_ge(s_split[v // N], 2)
                pe.wait_ge(d_xTl, v + 2)
                pair_T(B_qk2[:, 0:256], Wq, h, 2)
                pair_T(B_qk2[:, 256:512], Wk, h, 2).then_inc(p_qk2, 2)

            def q_T_01(v, p, h):
                if isinstance(v, int) and v in (0, N):
                    pe.wait_ge(s_split[v // N], 1)
                if have(v - 1):
                    pe.wait_ge(d_y0, v)
                elif have(v - 3):
                    pe.wait_ge(d_r1, v - 2)
                for f in range(2):
                    last = pair_T(B_q01[:, f * 256:(f + 1) * 256], Wq, h, f)
                last.then_inc(p_q01, 2)

            def k_T_01(v, p, h):
                if isinstance(v, int) and v in (0, N):
                    pe.wait_ge(s_split[v // N], 2)
                pe.wait_ge(a_qk2, v + 1)
                for f in range(2):
                    last = pair_T(B_k01[:, f * 256:(f + 1) * 256], Wk, h, f)
                last.then_inc(p_k01, 2)

            def scores(v, p, h):
                pe.wait_ge(a_nb, v + 1)
                pe.wait_ge(a_q01, v + 1)
                pe.wait_ge(a_k01, v + 1)
                for b in range(2):
                    mm(S[:, b * 512:b * 512 + 384], identb[:, :],
                       nb[:, :].unsqueeze(1).to_broadcast([128, 3, 128]), start=True, stop=False)
                for f in range(KT):
                    for b in range(2):
                        last = mm(S[:, b * 512 + f * 128:b * 512 + f * 128 + 128], qT[64 * b:64 * b + 64, f, p, :],
                                  kT[64 * b:64 * b + 64, f, p, :], start=False, stop=(f == KT - 1))
                last.then_inc(p_s, 1)

            def v_proj(v, p, h):
                pe.wait_ge(d_xTl, v + 1)
                if isinstance(v, int) and v in (0, N):
                    pe.wait_ge(s_split[v // N], 3)
                if p == 0:
                    if have(v - 1):
                        pe.wait_ge(d_yTl, v)
                    elif have(v - 3):
                        pe.wait_ge(d_o, v - 2)
                else:
                    pe.wait_ge(d_cTl, v)
                split3(B_v[p][:, 0:D], xTh[:, :, p, :], xTl[:, :, p, :], Wv, h).then_inc(p_v, 1)

            def period(do):
                do(4, y_T)
                do(3, probs_T, 1)
                do(3, probs_T, 0)
                do(5, logits, 1)
                do(4, h_proj)
                do(4, gate_proj)
                do(4, tanh_T)
                do(5, gat_probs_T, 0)
                do(5, gat_probs_T, 2)
                do(4, src_dst)
                do(3, context)
                do(5, gat_probs_T, 1)
                do(1, x_T)
                do(4, logits, 0)
                do(4, logits, 2)
                do(4, logits, 1)
                do(5, weighted_T)
                do(3, out_proj)
                do(5, o_back)
                do(2, qk_T_2)
                do(2, q_T_01)
                do(2, k_T_01)
                do(3, y_T)
                do(4, gat_probs_T, 0)
                do(2, scores)
                do(3, h_proj)
                do(2, v_proj)
                do(4, gat_probs_T, 1)
                do(3, tanh_T)
                do(4, gat_probs_T, 2)
                do(0, x_T)
                do(3, src_dst)
                do(2, probs_T, 0)
                do(4, weighted_T)
                do(2, probs_T, 1)
                do(3, logits, 0)
                do(4, o_back)
                do(2, context)
                do(1, scores)
                do(2, out_proj)
                do(3, logits, 2)
                do(1, v_proj)
                do(3, gate_proj)

            run(pe, period)

        @block.scalar
        def _(act):
            av = nc.scalar.activation

            def mask_not(v, p, h):
                act.wait_ge(s_adj[p], dmas(v, p))
                av(nota[:, p, :], adj[:, p, :], ACT.Copy, scale=-1.0, bias=1.0).then_inc(a_nota, 1)

            def q_out_01(v, p, h):
                act.wait_ge(p_q01, v + 1)
                for f in range(2):
                    last = av(qT[:, f, :, :], pairs(B_q01[:, f * 256:(f + 1) * 256]), ACT.Identity, bias=bq[:, h, f:f + 1])
                last.then_inc(a_q01, 2)

            def gat_exp(v, p, h, c):
                act.wait_ge(d_mG[c // 2], v + 1)
                if have(v - 1):
                    act.wait_ge(d_rG, v)
                for a in range(2 * c, 2 * c + 2):
                    last = av(L[:, a, :], L[:, a, :], ACT.Exp, bias=mG[:, a:a + 1], accum_out=lG[:, a:a + 1])
                last.then_inc(a_eG[c], 1)

            def k_out_01(v, p, h):
                act.wait_ge(p_k01, v + 1)
                for f in range(2):
                    last = av(kT[:, f, :, :], pairs(B_k01[:, f * 256:(f + 1) * 256]), ACT.Identity, bias=bk[:, h, f:f + 1])
                last.then_inc(a_k01, 2)

            def y_T_high(v, p, h):
                act.wait_ge(p_yT, v + 1)
                if have(v - 1):
                    act.wait_ge(p_g, v)
                av(yTh[:, :, :], t3(B_yT[p]), ACT.Copy).then_inc(a_yTh, 1)

            def gat_probs_T_out(v, p, h, t):
                act.wait_ge(p_ptG[t], v + 1)
                av(ptG[:, 4 * t:4 * t + 4, :], Z3[:, 4 * t:4 * t + 4, :], ACT.Copy).then_inc(a_ptG[t], 1)

            def att_exp(v, p, h, b):
                act.wait_ge(g_bT, v + 1)
                for s in range(3 * b, 3 * b + 3):
                    last = av(pT[:, s, :], S4[:, b, s % 3, :], ACT.Exp, bias=bT[:, s:s + 1], scale=DH ** -0.5,
                              accum_out=lT[:, s:s + 1])
                last.then_inc(a_eT[b], 1)

            def tanh_h(v, p, h):
                act.wait_ge(d_h, v + 1)
                av(th[:, :], B_h[p][:, 0:D], ACT.Tanh).then_inc(a_th, 1)

            def tanh_T_out(v, p, h):
                act.wait_ge(p_thT, v + 1)
                av(thT[:, :, :], t3(B_thT[p]), ACT.Copy).then_inc(a_thT, 1)

            def mask_bias(v, p, h):
                act.wait_ge(s_adj[p], dmas(v, p))
                av(nb[:, :], adj[:, p, :], ACT.Copy, scale=-NEG, bias=NEG).then_inc(a_nb, 1)

            def x_T_high(v, p, h):
                act.wait_ge(p_xT, v + 1)
                if have(v - 2):
                    act.wait_ge(p_v, v - 1)
                av(xTh[:, :, p, :], t3(B_xT[p]), ACT.Copy).then_inc(a_xTh, 1)

            def probs_T_out(v, p, h, b):
                act.wait_ge(p_ptT[b], v + 1)
                av(ptT[:, 3 * b:3 * b + 3, :], S4[:, b, :, :], ACT.Copy).then_inc(a_ptT[b], 1)

            def weighted_T_out(v, p, h):
                act.wait_ge(p_av, v + 1)
                av(oT[:, :, :], t3(B_av[p]), ACT.Copy).then_inc(a_oT, 1)

            def fifth(v, p, h, t):
                act.wait_ge(p_z[t], v + 1)
                av(zw[:, 4 * t:4 * t + 4, :], Z3[:, 4 * t:4 * t + 4, :], ACT.Copy, scale=0.2).then_inc(a_w[t], 1)

            def context_high(v, p, h):
                act.wait_ge(p_ctx, v + 1)
                av(cTh[:, :, :], t3(B_ctx[p]), ACT.Copy).then_inc(a_cTh, 1)

            def elu_exp(v, p, h):
                act.wait_ge(d_om, v + 1)
                av(oe[:, :], om[:, :], ACT.Exp).then_inc(a_e, 1)

            def gate_tanh(v, p, h):
                act.wait_ge(d_gb, v + 1)
                if have(v - 2):
                    act.wait_ge(g_ou, v - 1)
                av(gt[:, p, :], gb[:, :], ACT.Tanh, scale=0.5).then_inc(a_gt, 1)

            def qk_out_2(v, p, h):
                act.wait_ge(p_qk2, v + 1)
                av(qT[:, 2, :, :], pairs(B_qk2[:, 0:256]), ACT.Identity, bias=bq[:, h, 2:3])
                av(kT[:, 2, :, :], pairs(B_qk2[:, 256:512]), ACT.Identity, bias=bk[:, h, 2:3]).then_inc(a_qk2, 2)

            def period(do):
                do(3, mask_not)
                do(2, q_out_01)
                do(4, gat_exp, 2)
                do(2, k_out_01)
                do(3, y_T_high)
                do(4, gat_exp, 3)
                do(4, gat_probs_T_out, 0)
                do(4, gat_exp, 5)
                do(4, gat_exp, 4)
                do(2, att_exp, 1)
                do(3, tanh_h)
                do(2, att_exp, 0)
                do(3, tanh_T_out)
                do(4, gat_probs_T_out, 2)
                do(4, gat_probs_T_out, 1)
                do(1, mask_bias)
                do(0, x_T_high)
                do(2, probs_T_out, 0)
                do(4, weighted_T_out)
                do(2, probs_T_out, 1)
                do(3, fifth, 0)
                do(2, context_high)
                do(4, elu_exp)
                do(2, mask_not)
                do(1, att_exp, 1)
                do(1, att_exp, 0)
                do(3, fifth, 2)
                do(3, gat_exp, 0)
                do(2, y_T_high)
                do(3, gat_exp, 1)
                do(1, probs_T_out, 0)
                do(3, fifth, 1)
                do(1, probs_T_out, 1)
                do(3, gate_tanh)
                do(3, gat_exp, 4)
                do(2, tanh_h)
                do(3, gat_exp, 5)
                do(2, tanh_T_out)
                do(3, gat_exp, 3)
                do(3, gat_exp, 2)
                do(3, gat_probs_T_out, 0)
                do(3, gat_probs_T_out, 2)
                do(0, mask_bias)
                do(3, gat_probs_T_out, 1)
                do(1, context_high)
                do(-1, x_T_high)
                do(2, fifth, 0)
                do(2, fifth, 1)
                do(2, gate_tanh)
                do(3, weighted_T_out)
                do(2, gat_exp, 1)
                do(2, gat_exp, 0)
                do(2, fifth, 2)
                do(0, qk_out_2)
                do(3, elu_exp)

            run(act, period)

        @block.vector
        def _(dve):
            vec = nc.vector
            n_set = [0]

            def chained(ins):
                n_set[0] += 1
                ins.then_inc(s_pset, 1)
                dve.wait_ge(s_pset, n_set[0])

            def split_weight(c):
                i, w = c // 6, (Wq, Wk, Wv, Wf, Wg, Wh)[c % 6]
                dve.wait_ge(s_slot[c % 3], 16 * (c // 3 + 1))
                chained(vec.tensor_copy(w[0][:, i, :, :], slot[c % 3]))
                vec.tensor_tensor(w[1][:, i, :, :], slot[c % 3], w[0][:, i, :, :], ALU.subtract).then_inc(s_split[i], 1)

            def second_half(v, p, h):
                if isinstance(v, int) and v == 0:
                    for c in range(6, 12):
                        split_weight(c)

            dve.wait_ge(s_const, 16 * 5)
            chained(vec.tensor_copy(identb[:, :], ident[:, :]))
            chained(vec.tensor_copy(selb[:, :, :, :], bc(selc[:, :, :], 128)))
            chained(vec.memset(mhalf[:, :], -0.5))
            chained(vec.memset(threes[:, :], 3.0))
            chained(vec.memset(eighth[:, :], DH ** -0.5))
            for i in range(2):
                chained(vec.tensor_tensor(sdtmp[:, 0, :, :], sdmask[:, 0, :, :], bc(wsrc[:, i, :], 96), ALU.mult))
                chained(vec.tensor_tensor(sdtmp[:, 1, :, :], sdmask[:, 1, :, :], bc(wdst[:, i, :], 96), ALU.mult))
                chained(vec.tensor_tensor(Wsd[:, i, :, :], sdtmp[:, 0, :, :], sdtmp[:, 1, :, :], ALU.add))
            vec.memset(masked[:, :], -999.0).then_inc(s_setup, 1)
            for c in range(6):
                split_weight(c)
            dve.wait_ge(s_setup, 1)
            dve.wait_ge(s_split[0], 6)

            def leaky(v, p, h, t):
                dve.wait_ge(a_w[t], v + 1)
                vec.tensor_tensor(L[:, 4 * t:4 * t + 4, :], Z3[:, 4 * t:4 * t + 4, :], zw[:, 4 * t:4 * t + 4, :],
                                ALU.max).then_inc(d_L[t], 1)

            def gat_var_eps(v, p, h):
                dve.wait_ge(d_mv2, v + 1)
                vec.tensor_scalar(ve2[:, :], mv2[:, 1:2], 4.0 * EPS, None, ALU.add).then_inc(d_ve2, 1)

            def att_stats(v, p, h):
                dve.wait_ge(d_y0, v + 1)
                vec.bn_stats(st[:, :], y0[:, :]).then_inc(d_st, 1)

            def gat_divide(v, p, h):
                dve.wait_ge(p_o, v + 1)
                dve.wait_ge(d_rG, v + 1)
                vec.tensor_tensor(o[:, :].rearrange("p (a e) -> p a e", a=GH), B_o[p][:, 0:D].rearrange("p (a e) -> p a e", a=GH),
                                bc(rG[:, :], DG), ALU.mult).then_inc(d_o, 1)

            def mask(v, p, h, t):
                dve.wait_ge(s_setup, 1)
                dve.wait_ge(a_nota, v + 1)
                dve.wait_ge(d_L[t], v + 1)
                vec.copy_predicated(L[:, 4 * t:4 * t + 4, :], nota[:, p, :].unsqueeze(1).to_broadcast([128, 4, 128]),
                                  masked[:, :].unsqueeze(1).to_broadcast([128, 4, 128])).then_inc(d_pred[t], 1)

            def below_zero(v, p, h):
                dve.wait_ge(d_o, v + 1)
                vec.tensor_scalar(om[:, :], o[:, :], 0.0, None, ALU.min).then_inc(d_om, 1)

            def att_mean_var(v, p, h):
                dve.wait_ge(s_setup, 1)
                dve.wait_ge(d_st, v + 1)
                vec.bn_aggr(mv[:, :], st[:, :]).then_inc(d_mv, 1)

            def gat_max(v, p, h, t):
                dve.wait_ge(d_pred[t], v + 1)
                vec.tensor_reduce(mG[:, 4 * t:4 * t + 4], L[:, 4 * t:4 * t + 4, :], AX.X, ALU.max, negate=True).then_inc(d_mG[t], 1)

            def att_var_eps(v, p, h):
                dve.wait_ge(d_mv, v + 1)
                vec.tensor_scalar(ve[:, :], mv[:, 1:2], EPS, None, ALU.add).then_inc(d_ve, 1)

            def elu(v, p, h):
                dve.wait_ge(a_e, v + 1)
                vec.scalar_tensor_tensor(oq[:, :], o[:, :], 0.0, oe[:, :], ALU.max, ALU.add).then_inc(d_oq, 1)

            def elu_less_y(v, p, h):
                dve.wait_ge(d_oq, v + 1)
                vec.scalar_tensor_tensor(od[:, :], oq[:, :], 1.0, y[:, p, :], ALU.subtract, ALU.subtract).then_inc(d_od, 1)

            def att_norm(v, p, h):
                dve.wait_ge(g_rs, v + 1)
                if have(v - 2):
                    dve.wait_ge(d_od, v - 1)
                vec.tensor_scalar(y[:, p, :], y0[:, :], mv[:, 0:1], rs[:, :], ALU.subtract, ALU.mult).then_inc(d_y, 1)

            def y_T_low(v, p, h):
                dve.wait_ge(a_yTh, v + 1)
                vec.tensor_tensor(yTl[:, :, :], t3(B_yT[p]), yTh[:, :, :], ALU.subtract).then_inc(d_yTl, 1)

            def att_max(v, p, h):
                dve.wait_ge(p_s, v + 1)
                vec.tensor_reduce(mT[:, :].rearrange("p (b j) -> p b j", b=2), S4, AX.X, ALU.max, negate=True).then_inc(d_mT, 1)

            def gat_norm(v, p, h):
                dve.wait_ge(g_rs2, v + 1)
                if have(v - 2):
                    dve.wait_ge(s_st[p], dmas(v - 2, p))
                vec.tensor_scalar(res[:, p, :], os_[:, :], mv2[:, 0:1], rs2[:, :], ALU.subtract, ALU.mult).then_inc(d_res, 1)

            def h_bias(v, p, h):
                dve.wait_ge(p_h, v + 1)
                vec.tensor_tensor(ha[:, p, :].rearrange("p (a e) -> p a e", a=GH), B_h[p][:, 0:D].rearrange("p (a e) -> p a e", a=GH),
                                bg[:, h, :].unsqueeze(1).to_broadcast([128, GH, DG]), ALU.add).then_inc(d_h, 1)

            def att_reciprocal(v, p, h):
                dve.wait_ge(a_eT[0], v + 1)
                dve.wait_ge(a_eT[1], v + 1)
                vec.reciprocal(rT[:, :], lT[:, :]).then_inc(d_rT, 1)

            def v_bias(v, p, h):
                dve.wait_ge(p_v, v + 1)
                vec.tensor_tensor(va[:, :], B_v[p][:, 0:D], bv[:, h, :], ALU.add).then_inc(d_v, 1)

            def gated_sum(v, p, h):
                dve.wait_ge(g_op, v + 1)
                if have(v - 1):
                    dve.wait_ge(d_res, v)
                vec.scalar_tensor_tensor(os_[:, :], oq[:, :], 4.0, op[:, :], ALU.mult, ALU.add).then_inc(d_os, 1)

            def src_dst_first(v, p, h):
                dve.wait_ge(p_sd, v + 1)
                vec.tensor_copy(sd[:, :], B_sd[p][0:96, 0:128]).then_inc(d_hi, 1)

            def gat_reciprocal(v, p, h):
                dve.wait_ge(a_eG[0], v + 1)
                dve.wait_ge(a_eG[1], v + 1)
                dve.wait_ge(a_eG[2], v + 1)
                dve.wait_ge(a_eG[3], v + 1)
                dve.wait_ge(a_eG[4], v + 1)
                dve.wait_ge(a_eG[5], v + 1)
                vec.reciprocal(rG[:, :], lG[:, :]).then_inc(d_rG, 1)

            def src_dst_rest(v, p, h):
                dve.wait_ge(d_hi, v + 1)
                vec.tensor_tensor(sr[:, :], B_sd[p][0:96, 0:128], sd[:, :], ALU.subtract).then_inc(d_r1, 1)

            def src_dst_mid(v, p, h):
                dve.wait_ge(d_r1, v + 1)
                vec.tensor_copy(sm[:, :], sr[:, :]).then_inc(d_mid, 1)

            def src_dst_second(v, p, h):
                dve.wait_ge(d_r1, v + 1)
                vec.tensor_copy(sd[32:64, :], sr[32:64, :]).then_inc(d_sp1, 1)

            def src_dst_third(v, p, h):
                dve.wait_ge(d_mid, v + 1)
                dve.wait_ge(d_sp1, v + 1)
                vec.tensor_tensor(sd[64:96, :], sr[64:96, :], sm[64:96, :], ALU.subtract).then_inc(d_sd, 1)

            def x_T_low(v, p, h):
                dve.wait_ge(a_xTh, v + 1)
                vec.tensor_tensor(xTl[:, :, p, :], t3(B_xT[p]), xTh[:, :, p, :], ALU.subtract).then_inc(d_xTl, 1)

            def gat_stats(v, p, h):
                dve.wait_ge(d_os, v + 1)
                vec.bn_stats(st2[:, :], os_[:, :]).then_inc(d_st2, 1)

            def context_low(v, p, h):
                dve.wait_ge(a_cTh, v + 1)
                vec.tensor_tensor(cTl[:, :, :], t3(B_ctx[p]), cTh[:, :, :], ALU.subtract).then_inc(d_cTl, 1)

            def gat_mean_var(v, p, h):
                dve.wait_ge(s_setup, 1)
                dve.wait_ge(d_st2, v + 1)
                vec.bn_aggr(mv2[:, :], st2[:, :]).then_inc(d_mv2, 1)

            def att_sum(v, p, h):
                dve.wait_ge(p_f, v + 1)
                dve.wait_ge(g_xb, v + 1)
                vec.tensor_tensor(y0[:, :], B_f[p][:, 0:D], xb[:, :], ALU.add).then_inc(d_y0, 1)

            def gate_bias(v, p, h):
                dve.wait_ge(p_g, v + 1)
                if have(v - 1):
                    dve.wait_ge(a_gt, v)
                vec.tensor_tensor(gb[:, :], B_g[p][:, 0:D], bh[:, h, :], ALU.add).then_inc(d_gb, 1)

            def period(do):
                do(4, leaky, 1)
                do(6, gat_var_eps)
                do(3, att_stats)
                do(5, gat_divide)
                do(4, mask, 1)
                do(5, below_zero)
                do(3, att_mean_var)
                do(4, gat_max, 1)
                do(3, att_var_eps)
                do(5, elu)
                do(5, elu_less_y)
                do(3, att_norm)
                do(4, leaky, 2)
                do(4, mask, 2)
                do(3, y_T_low)
                do(4, gat_max, 2)
                do(2, att_max)
                do(6, gat_norm)
                do(3, h_bias)
                do(2, att_reciprocal)
                do(2, v_bias)
                do(5, gated_sum)
                do(3, src_dst_first)
                do(4, gat_reciprocal)
                do(3, src_dst_rest)
                do(3, src_dst_mid)
                do(3, src_dst_second)
                do(3, src_dst_third)
                do(0, x_T_low)
                do(5, gat_stats)
                do(4, gat_divide)
                do(3, leaky, 0)
                do(4, below_zero)
                do(2, context_low)
                do(3, mask, 0)
                do(1, att_max)
                do(5, gat_mean_var)
                do(4, elu)
                do(2, att_sum)
                do(2, att_stats)
                do(5, gat_var_eps)
                do(2, att_mean_var)
                do(4, elu_less_y)
                do(2, att_var_eps)
                do(3, gat_max, 0)
                do(1, att_reciprocal)
                do(2, att_norm)
                do(3, leaky, 2)
                do(3, gate_bias)
                do(2, y_T_low)
                do(3, mask, 2)
                do(3, gat_max, 2)
                do(3, leaky, 1)
                do(2, h_bias)
                do(3, mask, 1)
                do(3, gat_max, 1)
                do(1, v_bias)
                do(5, gat_norm)
                do(2, gate_bias)
                do(2, src_dst_first)
                do(2, src_dst_rest)
                do(2, src_dst_second)
                do(2, src_dst_mid)
                do(2, src_dst_third)
                do(4, gated_sum)
                do(4, gat_stats)
                do(3, gat_reciprocal)
                do(1, context_low)
                do(-1, x_T_low)
                do(2, leaky, 0)
                do(2, mask, 0)
                do(2, gat_max, 0)
                do(4, gat_mean_var)
                do(1, att_sum)
                do(0, second_half)

            run(dve, period)

        @block.gpsimd
        def _(pool):
            g = nc.gpsimd
            pool.wait_ge(s_setup, 1)

            def att_divide(v, p, h, b):
                pool.wait_ge(d_rT, v + 1)
                g.tensor_tensor(pT[:, 3 * b:3 * b + 3, :], pT[:, 3 * b:3 * b + 3, :], bc(rT[:, 3 * b:3 * b + 3], 128),
                                ALU.mult).then_inc(g_pn[b], 1)

            def gate_product(v, p, h):
                pool.wait_ge(d_od, v + 1)
                pool.wait_ge(g_ou, v + 1)
                g.tensor_tensor(op[:, :], op[:, :], od[:, :], ALU.mult).then_inc(g_op, 1)

            def residual(v, p, h):
                pool.wait_ge(s_x[p], dmas(v, p))
                g.tensor_tensor(xb[:, :], x[:, p, :], bf[:, h, :], ALU.add).then_inc(g_xb, 1)

            def tanh_less_3(v, p, h):
                pool.wait_ge(a_gt, v + 1)
                if have(v - 1):
                    pool.wait_ge(d_os, v)
                g.tensor_tensor(op[:, :], gt[:, p, :], threes[:, :].to_broadcast([128, D]), ALU.subtract).then_inc(g_ou, 1)

            def att_rstd(v, p, h):
                pool.wait_ge(d_ve, v + 1)
                g.tensor_tensor(rs[:, :], ve[:, :], mhalf[:, :], ALU.pow).then_inc(g_rs, 1)

            def gat_rstd(v, p, h):
                pool.wait_ge(d_ve2, v + 1)
                g.tensor_tensor(rs2[:, :], ve2[:, :], mhalf[:, :], ALU.pow).then_inc(g_rs2, 1)

            def att_max_scaled(v, p, h):
                pool.wait_ge(d_mT, v + 1)
                g.tensor_tensor(bT[:, :], mT[:, :], eighth[:, :], ALU.mult).then_inc(g_bT, 1)

            def period(do):
                do(1, att_divide, 0)
                do(4, gate_product)
                do(1, residual)
                do(3, tanh_less_3)
                do(1, att_rstd)
                do(4, gat_rstd)
                do(0, residual)
                do(3, gate_product)
                do(0, att_max_scaled)
                do(0, att_divide, 0)
                do(0, att_divide, 1)
                do(2, tanh_less_3)
                do(-1, att_max_scaled)
                do(3, gat_rstd)
                do(0, att_rstd)
                do(-1, att_divide, 1)

            run(pool, period)


def kernel(**inputs):
    import numpy as np
    import concourse.bacc as bacc
    from concourse.bass_utils import run_bass_kernel_spmd

    N = NGRAPH
    nc = bacc.Bacc("TRN2", target_bir_lowering=False, num_devices=1)
    arrays = {}
    for name, a in inputs.items():
        a = np.asarray(a)
        if name.endswith("H_w"):
            a = a.T
        if name.endswith("gnn_W"):
            a = a.transpose(1, 0, 2).reshape(384, 384)
        arrays[name] = np.ascontiguousarray(a)
    col = lambda a: a.reshape(3, 128).T
    take = lambda i, n: arrays.pop(f"L{i}_gnn_{n}")
    arrays["cols"] = np.ascontiguousarray(np.stack(
        [np.stack([col(take(*w)) for w in ((2 * i, "bq"), (2 * i, "bk"), (2 * i + 1, "w_src"), (2 * i + 1, "w_dst"))], 1)
         for i in range(2)], 1).reshape(128, -1))
    arrays["rows"] = np.concatenate([take(*w) for i in range(2) for w in (
        (2 * i, "bv"), (2 * i, "bf"), (2 * i + 1, "H_b"), (2 * i + 1, "b"))])
    arrays = {"in_" + n: a for n, a in arrays.items()}
    arrays.update({"in_" + n: a for n, a in _consts().items()})
    aps = {n[3:]: nc.dram_tensor(n, a.shape, mybir.dt.from_np(a.dtype), kind="ExternalInput").ap()
           for n, a in arrays.items()}
    mid = nc.dram_tensor("mid", (N, 128, 384), mybir.dt.float32, kind="Internal").ap()
    out = nc.dram_tensor("out", (N, 128, 384), mybir.dt.float32, kind="ExternalOutput").ap()
    build(nc, N, aps, mid, out)
    r = run_bass_kernel_spmd(nc, [arrays], core_ids=[0])
    return r.results[0]["out"]
```

```python
import concourse.bass as bass
from concourse import mybir
from contextlib import ExitStack

NGRAPH = 128


def _consts():
    import numpy as np
    ident = np.eye(128, dtype=np.float32)
    sel = np.zeros((96, 2, 12), np.float32)
    sd = np.zeros((128, 2, 3, 96), np.float32)
    for g in range(3):
        for a in range(12):
            sel[32 * g + a, 0, a] = 1.0
            sel[32 * g + 12 + a, 1, a] = 1.0
            sd[32 * (a % 4):32 * (a % 4) + 32, 0, a // 4, 32 * g + a] = 1.0
            sd[32 * (a % 4):32 * (a % 4) + 32, 1, a // 4, 32 * g + 12 + a] = 1.0
    return {"c_ident": ident, "c_sel": sel, "c_sd": sd.reshape(128, -1)}


def build(nc, N, I, mid, out):
    f32, f32r, bf16, u8 = mybir.dt.float32, mybir.dt.float32r, mybir.dt.bfloat16, mybir.dt.uint8
    ALU, ACT, AX = mybir.AluOpType, mybir.ActivationFunctionType, mybir.AxisListType

    D, KT = 384, 3
    AH, DH = 6, 64
    GH, DG = 12, 32
    NEG = -9000000000000000.0 * 8.0
    EPS = 1e-5
    U = 2 * N
    EDGE = 10

    ctx = ExitStack()
    with ctx:
        def sb(name, shape, dt=f32):
            return ctx.enter_context(nc.sbuf_tensor(name, shape, dt))

        def sem(name):
            return ctx.enter_context(nc.semaphore(name))

        def sems(name, n):
            return [sem(f"{name}{i}") for i in range(n)]

        Z = ctx.enter_context(nc.psum_tensor("Z", [128, GH * 128], f32))
        S = ctx.enter_context(nc.psum_tensor("S", [128, 1024], f32))
        W = [ctx.enter_context(nc.psum_tensor(f"W{i}", [128, 512], f32)) for i in range(3)]

        Wq, Wk, Wv, Wf, Wg, Wh = [(sb(n + "h", [128, 2, KT, D], f32r), sb(n + "l", [128, 2, KT, D], f32r))
                          for n in ("Wq", "Wk", "Wv", "Wf", "Wg", "Wh")]
        cols = sb("cols", [128, 2, 4, KT])
        bq, bk, wsrc, wdst = (cols[:, :, c, :] for c in range(4))
        rows = sb("rows", [128, 2, KT * D + DG])
        bv, bf, bh = (rows[:, :, c * D:(c + 1) * D] for c in range(3))
        bg = rows[:, :, 3 * D:3 * D + DG]
        Wsd = sb("Wsd", [128, 2, KT, 96])
        ident = sb("ident", [128, 128])
        identb = sb("identb", [128, 128], bf16)
        selc = sb("selc", [96, 2, GH])
        selb = sb("selb", [96, 2, GH, 128], bf16)
        masked = sb("masked", [128, 1])
        mhalf = sb("mhalf", [128, 1])
        eighth = sb("eighth", [128, AH])
        threes = sb("threes", [128, 1])

        x = sb("x", [128, 2, D])
        adj = sb("adj", [128, 2, 128], u8)
        nota = sb("nota", [128, 2, 128], u8)
        nb = sb("nb", [128, 128], bf16)
        xb = sb("xb", [128, D])
        xTh, xTl = sb("xTh", [128, KT, 2, 128], f32r), sb("xTl", [128, KT, 2, 128], f32r)
        qT, kT = sb("qT", [128, KT, 2, 128]), sb("kT", [128, KT, 2, 128])
        va = sb("va", [128, D])
        mT = sb("mT", [128, AH])
        pT = sb("pT", [128, AH, 128])
        ptT = sb("ptT", [128, AH, 128])
        bT, lT, rT = sb("bT", [128, AH]), sb("lT", [128, AH]), sb("rT", [128, AH])
        cTh, cTl = sb("cTh", [128, KT, 128], f32r), sb("cTl", [128, KT, 128], f32r)
        y0 = sb("y0", [128, D])
        y = sb("y", [128, 2, D])
        st, mv, ve, rs = sb("st", [128, 6]), sb("mv", [128, 2]), sb("ve", [128, 1]), sb("rs", [128, 1])
        yTh, yTl = sb("yTh", [128, KT, 128], f32r), sb("yTl", [128, KT, 128], f32r)
        ha = sb("ha", [128, 2, D])
        th = sb("th", [128, D])
        gb = sb("gb", [128, D])
        gt = sb("gt", [128, 2, D])
        thT = sb("thT", [128, KT, 128])
        sd = sb("sd", [96, 128], bf16)
        sr = sb("sr", [96, 128])
        sm = sb("sm", [96, 128], bf16)
        zw = sb("zw", [128, GH, 128])
        L = sb("L", [128, GH, 128])
        mG = sb("mG", [128, GH])
        ptG = sb("ptG", [128, GH, 128])
        lG, rG = sb("lG", [128, GH]), sb("rG", [128, GH])
        flat = lambda ap: ap[:, :, :].rearrange("p a m -> p (a m)")
        sdmask, sdtmp = (flat(b_)[:, 0:2 * KT * 96].rearrange("p (s t c) -> p s t c", s=2, t=KT) for b_ in (pT, ptT))
        slot = [flat(b_)[:, 0:KT * D].rearrange("p (t n) -> p t n", t=KT) for b_ in (zw, L, ptG)]
        oT = sb("oT", [128, KT, 128])
        o, om, oe, oq, od, op, os_ = [sb(n, [128, D]) for n in ("o", "om", "oe", "oq", "od", "op", "os")]
        st2, mv2, ve2, rs2 = sb("st2", [128, 6]), sb("mv2", [128, 2]), sb("ve2", [128, 1]), sb("rs2", [128, 1])
        res = sb("res", [128, 2, D])

        s_const = sem("s_const")
        s_slot = sems("s_slot", 3)
        s_split = sems("s_split", 2)
        s_x, s_adj, s_st = sems("s_x", 2), sems("s_adj", 2), sems("s_st", 2)
        s_setup, s_pset = sem("s_setup"), sem("s_pset")
        p_xT, p_q01, p_k01, p_qk2, p_v, p_s, p_ctx, p_f = (sem("p_" + n) for n in "xT q01 k01 qk2 v s ctx f".split())
        p_yT, p_h, p_g, p_thT, p_sd, p_av, p_o = (sem("p_" + n) for n in "yT h g thT sd av o".split())
        p_z, p_ptG, p_ptT = sems("p_z", 3), sems("p_ptG", 3), sems("p_ptT", 2)
        a_xTh, a_cTh, a_yTh, a_th, a_gt, a_thT, a_oT, a_e = (
            sem("a_" + n) for n in "xTh cTh yTh th gt thT oT e".split())
        a_nb, a_nota = sem("a_nb"), sem("a_nota")
        a_q01, a_k01, a_qk2 = sem("a_q01"), sem("a_k01"), sem("a_qk2")
        a_w, a_ptG = sems("a_w", 3), sems("a_ptG", 3)
        a_eG, a_eT, a_ptT = sems("a_eG", 6), sems("a_eT", 2), sems("a_ptT", 2)
        d_xTl, d_yTl, d_cTl, d_v, d_mT, d_rT = (sem("d_" + n) for n in "xTl yTl cTl v mT rT".split())
        d_y0, d_st, d_mv, d_ve, d_y = (sem("d_" + n) for n in "y0 st mv ve y".split())
        d_h, d_gb, d_hi, d_r1, d_mid, d_sp1, d_sd = (sem("d_" + n) for n in "h gb hi r1 mid sp1 sd".split())
        d_L, d_pred, d_mG = sems("d_L", 3), sems("d_pred", 3), sems("d_mG", 3)
        d_rG, d_o, d_om, d_oq, d_od, d_os, d_st2, d_mv2, d_ve2, d_res = (
            sem("d_" + n) for n in "rG o om oq od os st2 mv2 ve2 res".split())
        g_xb, g_rs, g_rs2, g_bT, g_op, g_ou = (sem("g_" + n) for n in "xb rs rs2 bT op ou".split())
        g_pn = sems("g_pn", 2)

        B_xT, B_f, B_o, B_v = (W[1], W[0]), (W[0], W[2]), (W[1], W[0]), (W[1], W[2])
        B_yT, B_h, B_g, B_thT = (W[0], W[1]), (W[1], W[1]), (W[0], W[2]), (W[1], W[0])
        B_sd, B_ctx, B_av = (W[1], W[0]), (W[0], W[2]), (W[2], W[1])
        B_q01, B_k01, B_qk2 = W[1], W[2], W[0]
        pairs = lambda ap: ap.rearrange("p (e n) -> p e n", e=2)
        S4 = S[:, :].rearrange("p (b c) -> p b c", b=2)[:, :, 0:384].rearrange("p b (j k) -> p b j k", j=3)
        Z3 = Z[:, :].rearrange("p (a m) -> p a m", m=128)
        t3 = lambda ap: ap[:, 0:D].rearrange("p (t n) -> p t n", t=KT)
        bc = lambda ap, n: ap.unsqueeze(len(ap.shape)).to_broadcast(list(ap.shape) + [n])

        def have(u):
            return not isinstance(u, int) or 0 <= u < U

        def dmas(u, par):
            return 8 * u + 16 - 8 * par

        def run(eng, period):
            def doer(u, half):
                def do(lag, stage, *args):
                    if half is not None or have(u - lag):
                        stage(u - lag if lag else u, lag % 2, (u - lag) // N if half is None else half, *args)
                return do

            for lo, hi, loop in ((0, EDGE, 0), (EDGE, N, 1), (N, N + EDGE, 0), (N + EDGE, U, 1), (U, U + EDGE, 0)):
                if loop and hi > lo:
                    with eng.Fori(lo, hi - 1, 2) as u:
                        period(doer(u, lo // N))
                else:
                    for u in range(lo, hi, 2):
                        period(doer(u, None))

        block = ctx.enter_context(nc.Block())

        @block.sync
        def _(sp):
            for dst, src in ((ident[:, :], I["c_ident"]), (selc[:, :, :], I["c_sel"]),
                             (flat(pT)[:, 0:2 * KT * 96], I["c_sd"]),
                             (cols[:, :, :, :].rearrange("p i c t -> p (i c t)"), I["cols"]),
                             (rows[:, :, :].rearrange("p i n -> p (i n)"), I["rows"].partition_broadcast(128))):
                sp.dma_start(dst, src).then_inc(s_const, 16)

            def weight(c):
                i, n = c // 6, c % 6
                A_, G_ = f"L{2 * i}_gnn_", f"L{2 * i + 1}_gnn_"
                w = (A_ + "Wq", A_ + "Wk", A_ + "Wv", A_ + "Wf", G_ + "W", G_ + "H_w")[n]
                if c >= 3:
                    sp.wait_ge(s_split[(c - 3) // 6], (c - 3) % 6 + 1)
                sp.dma_start(slot[c % 3], I[w].rearrange("(t p) n -> p t n", p=128)).then_inc(s_slot[c % 3], 16)

            def load_x(v, p, h):
                sp.wait_ge(s_const, 16 * 5)
                if have(v - 2):
                    sp.wait_ge(g_xb, v - 1)
                    sp.wait_ge(p_xT, v - 1)
                if h == 1:
                    sp.wait_ge(s_st[p], dmas(v - N, p))
                sp.dma_start(x[:, p, :], I["x"][v, :, :] if h == 0 else mid[v - N, :, :]).then_inc(s_x[p], 16)

            def load_adj(v, p, h):
                sp.wait_ge(s_const, 16 * 5)
                if have(v - 2):
                    sp.wait_ge(a_nota, v - 1)
                    sp.wait_ge(a_nb, v - 1)
                sp.dma_start(adj[:, p, :], I["adj"][v - h * N, :, :]).then_inc(s_adj[p], 16)

            def store(v, p, h):
                sp.wait_ge(s_const, 16 * 5)
                sp.wait_ge(d_res, v + 1)
                sp.dma_start(mid[v, :, :] if h == 0 else out[v - N, :, :], res[:, p, :]).then_inc(s_st[p], 16)

            def weights(v, p, h):
                if isinstance(v, int) and v == 0:
                    for c in range(12):
                        weight(c)

            def period(do):
                do(0, load_x)
                do(6, store)
                do(-1, load_x)
                do(0, weights)
                do(0, load_adj)
                do(5, store)
                do(-1, load_adj)

            run(sp, period)
            for par in range(2):
                sp.wait_ge(s_st[par], dmas(U - 2 + par, par))

        @block.tensor
        def _(pe):
            mm, tr = nc.tensor.matmul, nc.tensor.transpose
            pe.wait_ge(s_setup, 1)

            def pair_T(ps, w, i, f):
                for t in range(KT):
                    wh, wl = (w[c][:, i, t, f * 128:(f + 1) * 128] for c in range(2))
                    mm(ps, wh, xTh[:, t, :, :], start=(t == 0), stop=False)
                    mm(ps, wh, xTl[:, t, :, :], start=False, stop=False)
                    last = mm(ps, wl, xTh[:, t, :, :], start=False, stop=(t == KT - 1))
                return last

            def split3(ps, xh, xl, w, i):
                for t in range(KT):
                    mm(ps, xh[:, t, :], w[0][:, i, t, :], start=(t == 0), stop=False)
                    mm(ps, xh[:, t, :], w[1][:, i, t, :], start=False, stop=False)
                    last = mm(ps, xl[:, t, :], w[0][:, i, t, :], start=False, stop=(t == KT - 1))
                return last

            def probs_T(v, p, h, b):
                pe.wait_ge(g_pn[b], v + 1)
                for i in range(3):
                    last = tr(S4[:, b, i, :], pT[:, 3 * b + i, :], ident[:, :])
                last.then_inc(p_ptT[b], 1)

            def weighted_T(v, p, h):
                pe.wait_ge(a_ptG[0], v + 1)
                pe.wait_ge(a_ptG[1], v + 1)
                pe.wait_ge(a_ptG[2], v + 1)
                if p == 0:
                    pe.wait_ge(d_gb, v + 2)
                else:
                    if have(v + 1):
                        pe.wait_ge(d_r1, v + 2)
                    elif have(v + 3):
                        pe.wait_ge(a_q01, v + 4)
                    else:
                        pe.wait_ge(d_o, v)
                for t in range(3):
                    for i in range(4):
                        a = 4 * t + i
                        last = mm(B_av[p][32 * i:32 * i + 32, t * 128:(t + 1) * 128], ha[:, p, a * DG:(a + 1) * DG],
                                  ptG[:, a, :], start=True, stop=True)
                last.then_inc(p_av, 1)

            def x_T(v, p, h):
                pe.wait_ge(s_x[p], dmas(v, p))
                if p == 0:
                    if have(v - 3):
                        pe.wait_ge(a_th, v - 2)
                    elif have(v - 2):
                        pe.wait_ge(d_v, v - 1)
                    elif have(v - 5):
                        pe.wait_ge(a_oT, v - 4)
                else:
                    if have(v - 4):
                        pe.wait_ge(d_r1, v - 3)
                    elif have(v - 3):
                        pe.wait_ge(d_y0, v - 2)
                    elif have(v - 6):
                        pe.wait_ge(d_o, v - 5)
                for t in range(KT):
                    last = tr(B_xT[p][:, t * 128:(t + 1) * 128], x[:, p, t * 128:(t + 1) * 128], ident[:, :])
                last.then_inc(p_xT, 1)

            def logits(v, p, h, t):
                pe.wait_ge(d_sd, v + 1)
                if have(v - 1):
                    pe.wait_ge(a_ptG[t], v)
                mm(Z[:, t * 512:(t + 1) * 512], sd[:, :], selb[:, 0, 4 * t:4 * t + 4, :], start=True, stop=False)
                for a in range(4 * t, 4 * t + 4):
                    last = mm(Z3[:, a, :], selb[:, 1, a, :], sd[:, :], start=False, stop=(a == 4 * t + 3))
                last.then_inc(p_z[t], 1)

            def o_back(v, p, h):
                pe.wait_ge(a_oT, v + 1)
                if p == 0:
                    if have(v + 4):
                        pe.wait_ge(d_xTl, v + 5)
                    else:
                        pe.wait_ge(a_th, v + 2)
                else:
                    if have(v + 1):
                        pe.wait_ge(d_gb, v + 2)
                    elif have(v + 3):
                        pe.wait_ge(a_qk2, v + 4)
                    else:
                        pe.wait_ge(d_r1, v + 1)
                for t in range(KT):
                    last = tr(B_o[p][:, t * 128:(t + 1) * 128], oT[:, t, :], ident[:, :])
                last.then_inc(p_o, 1)

            def qk_T_2(v, p, h):
                pe.wait_ge(d_xTl, v + 2)
                if isinstance(v, int) and v in (0, N):
                    pe.wait_ge(s_split[v // N], 2)
                pe.wait_ge(d_xTl, v + 2)
                pair_T(B_qk2[:, 0:256], Wq, h, 2)
                pair_T(B_qk2[:, 256:512], Wk, h, 2).then_inc(p_qk2, 2)

            def context(v, p, h):
                pe.wait_ge(a_ptT[0], v + 1)
                pe.wait_ge(a_ptT[1], v + 1)
                pe.wait_ge(d_v, v + 1)
                if p == 0:
                    if have(v - 3):
                        pe.wait_ge(d_o, v - 2)
                    elif have(v - 2):
                        pe.wait_ge(d_gb, v - 1)
                    else:
                        pe.wait_ge(a_qk2, v + 1)
                else:
                    if have(v - 3):
                        pe.wait_ge(a_oT, v - 2)
                    else:
                        pe.wait_ge(d_v, v + 1)
                for f in range(KT):
                    for b in range(2):
                        a = 2 * f + b
                        last = mm(B_ctx[p][64 * b:64 * b + 64, f * 128:(f + 1) * 128], va[:, a * DH:(a + 1) * DH],
                                  ptT[:, 3 * b + f, :], start=True, stop=True)
                last.then_inc(p_ctx, 1)

            def q_T_01(v, p, h):
                if isinstance(v, int) and v in (0, N):
                    pe.wait_ge(s_split[v // N], 1)
                if have(v - 4):
                    pe.wait_ge(d_o, v - 3)
                else:
                    pe.wait_ge(d_xTl, v + 1)
                for f in range(2):
                    last = pair_T(B_q01[:, f * 256:(f + 1) * 256], Wq, h, f)
                last.then_inc(p_q01, 2)

            def y_T(v, p, h):
                pe.wait_ge(d_y, v + 1)
                if p == 0:
                    if have(v + 2):
                        pe.wait_ge(a_qk2, v + 3)
                    elif have(v - 1):
                        pe.wait_ge(d_r1, v)
                    else:
                        pe.wait_ge(d_y0, v + 1)
                else:
                    if have(v + 1):
                        pe.wait_ge(d_v, v + 2)
                    elif have(v - 2):
                        pe.wait_ge(a_oT, v - 1)
                    else:
                        pe.wait_ge(d_r1, v)
                for t in range(KT):
                    last = tr(B_yT[p][:, t * 128:(t + 1) * 128], y[:, p, t * 128:(t + 1) * 128], ident[:, :])
                last.then_inc(p_yT, 1)

            def k_T_01(v, p, h):
                if isinstance(v, int) and v in (0, N):
                    pe.wait_ge(s_split[v // N], 2)
                if have(v - 1):
                    pe.wait_ge(d_cTl, v)
                elif have(v - 4):
                    pe.wait_ge(a_oT, v - 3)
                for f in range(2):
                    last = pair_T(B_k01[:, f * 256:(f + 1) * 256], Wk, h, f)
                last.then_inc(p_k01, 2)

            def h_proj(v, p, h):
                pe.wait_ge(d_yTl, v + 1)
                if isinstance(v, int) and v in (0, N):
                    pe.wait_ge(s_split[v // N], 5)
                if p == 0:
                    if have(v + 2):
                        pe.wait_ge(a_q01, v + 3)
                    elif have(v - 2):
                        pe.wait_ge(d_o, v - 1)
                    else:
                        pe.wait_ge(d_v, v + 1)
                else:
                    pe.wait_ge(d_yTl, v + 1)
                split3(B_h[p][:, 0:D], yTh, yTl, Wg, h).then_inc(p_h, 1)

            def out_proj(v, p, h):
                pe.wait_ge(d_cTl, v + 1)
                if isinstance(v, int) and v in (0, N):
                    pe.wait_ge(s_split[v // N], 4)
                if p == 0:
                    pe.wait_ge(d_cTl, v + 1)
                else:
                    if have(v + 1):
                        pe.wait_ge(a_k01, v + 2)
                    else:
                        pe.wait_ge(d_cTl, v + 1)
                split3(B_f[p][:, 0:D], cTh, cTl, Wf, h).then_inc(p_f, 1)

            def tanh_T(v, p, h):
                pe.wait_ge(a_th, v + 1)
                if p == 0:
                    pe.wait_ge(a_th, v + 1)
                else:
                    if have(v + 1):
                        pe.wait_ge(d_y0, v + 2)
                    elif have(v - 2):
                        pe.wait_ge(d_o, v - 1)
                    else:
                        pe.wait_ge(d_gb, v)
                for t in range(KT):
                    last = tr(B_thT[p][:, t * 128:(t + 1) * 128], th[:, t * 128:(t + 1) * 128], ident[:, :])
                last.then_inc(p_thT, 1)

            def scores(v, p, h):
                pe.wait_ge(a_nb, v + 1)
                pe.wait_ge(a_q01, v + 1)
                pe.wait_ge(a_k01, v + 1)
                pe.wait_ge(a_qk2, v + 1)
                for b in range(2):
                    mm(S[:, b * 512:b * 512 + 384], identb[:, :],
                       nb[:, :].unsqueeze(1).to_broadcast([128, 3, 128]), start=True, stop=False)
                for f in range(KT):
                    for b in range(2):
                        last = mm(S[:, b * 512 + f * 128:b * 512 + f * 128 + 128], qT[64 * b:64 * b + 64, f, p, :],
                                  kT[64 * b:64 * b + 64, f, p, :], start=False, stop=(f == KT - 1))
                last.then_inc(p_s, 1)

            def gat_probs_T(v, p, h, t):
                pe.wait_ge(a_eG[2 * t], v + 1)
                pe.wait_ge(a_eG[2 * t + 1], v + 1)
                for a in range(4 * t, 4 * t + 4):
                    last = tr(Z3[:, a, :], L[:, a, :], ident[:, :])
                last.then_inc(p_ptG[t], 1)

            def src_dst(v, p, h):
                pe.wait_ge(a_thT, v + 1)
                for t in range(KT):
                    last = mm(B_sd[p][0:96, 0:128], Wsd[:, h, t, :], thT[:, t, :], start=(t == 0), stop=(t == KT - 1))
                last.then_inc(p_sd, 1)

            def gate_proj(v, p, h):
                if isinstance(v, int) and v in (0, N):
                    pe.wait_ge(s_split[v // N], 6)
                if p == 0:
                    pe.wait_ge(d_yTl, v + 1)
                else:
                    if have(v + 2):
                        pe.wait_ge(d_v, v + 3)
                    else:
                        pe.wait_ge(d_y0, v + 1)
                split3(B_g[p][:, 0:D], yTh, yTl, Wh, h).then_inc(p_g, 1)

            def v_proj(v, p, h):
                pe.wait_ge(d_xTl, v + 1)
                if isinstance(v, int) and v in (0, N):
                    pe.wait_ge(s_split[v // N], 3)
                if p == 0:
                    if have(v - 3):
                        pe.wait_ge(a_oT, v - 2)
                    elif have(v - 2):
                        pe.wait_ge(d_r1, v - 1)
                    else:
                        pe.wait_ge(a_q01, v + 1)
                else:
                    if have(v - 2):
                        pe.wait_ge(d_y0, v - 1)
                    else:
                        pe.wait_ge(a_k01, v)
                split3(B_v[p][:, 0:D], xTh[:, :, p, :], xTl[:, :, p, :], Wv, h).then_inc(p_v, 1)

            def period(do):
                do(3, probs_T, 1)
                do(6, weighted_T)
                do(1, x_T)
                do(5, logits, 1)
                do(5, logits, 2)
                do(6, o_back)
                do(5, logits, 0)
                do(2, qk_T_2)
                do(3, context)
                do(2, q_T_01)
                do(4, y_T)
                do(2, k_T_01)
                do(4, h_proj)
                do(3, out_proj)
                do(4, tanh_T)
                do(2, scores)
                do(5, gat_probs_T, 2)
                do(5, gat_probs_T, 0)
                do(4, src_dst)
                do(5, gat_probs_T, 1)
                do(4, gate_proj)
                do(4, logits, 2)
                do(5, weighted_T)
                do(4, logits, 0)
                do(4, logits, 1)
                do(5, o_back)
                do(2, v_proj)
                do(2, probs_T, 1)
                do(2, probs_T, 0)
                do(1, v_proj)
                do(2, context)
                do(1, scores)
                do(3, y_T)
                do(4, gat_probs_T, 2)
                do(2, out_proj)
                do(3, h_proj)
                do(3, gate_proj)
                do(3, tanh_T)
                do(4, gat_probs_T, 0)
                do(0, x_T)
                do(4, gat_probs_T, 1)
                do(3, src_dst)
                do(1, probs_T, 0)

            run(pe, period)

        @block.scalar
        def _(act):
            av = nc.scalar.activation

            def probs_T_out(v, p, h, b):
                act.wait_ge(p_ptT[b], v + 1)
                av(ptT[:, 3 * b:3 * b + 3, :], S4[:, b, :, :], ACT.Copy).then_inc(a_ptT[b], 1)

            def x_T_high(v, p, h):
                act.wait_ge(p_xT, v + 1)
                av(xTh[:, :, p, :], t3(B_xT[p]), ACT.Copy).then_inc(a_xTh, 1)

            def weighted_T_out(v, p, h):
                act.wait_ge(p_av, v + 1)
                av(oT[:, :, :], t3(B_av[p]), ACT.Copy).then_inc(a_oT, 1)

            def fifth(v, p, h, t):
                act.wait_ge(p_z[t], v + 1)
                av(zw[:, 4 * t:4 * t + 4, :], Z3[:, 4 * t:4 * t + 4, :], ACT.Copy, scale=0.2).then_inc(a_w[t], 1)

            def elu_exp(v, p, h):
                act.wait_ge(d_om, v + 1)
                av(oe[:, :], om[:, :], ACT.Exp).then_inc(a_e, 1)

            def qk_out_2(v, p, h):
                act.wait_ge(p_qk2, v + 1)
                av(qT[:, 2, :, :], pairs(B_qk2[:, 0:256]), ACT.Identity, bias=bq[:, h, 2:3])
                av(kT[:, 2, :, :], pairs(B_qk2[:, 256:512]), ACT.Identity, bias=bk[:, h, 2:3]).then_inc(a_qk2, 2)

            def context_high(v, p, h):
                act.wait_ge(p_ctx, v + 1)
                av(cTh[:, :, :], t3(B_ctx[p]), ACT.Copy).then_inc(a_cTh, 1)

            def mask_not(v, p, h):
                act.wait_ge(s_adj[p], dmas(v, p))
                if have(v - 2):
                    act.wait_ge(d_pred[1], v - 1)
                av(nota[:, p, :], adj[:, p, :], ACT.Copy, scale=-1.0, bias=1.0).then_inc(a_nota, 1)

            def gat_exp(v, p, h, c):
                act.wait_ge(d_mG[c // 2], v + 1)
                for a in range(2 * c, 2 * c + 2):
                    last = av(L[:, a, :], L[:, a, :], ACT.Exp, bias=mG[:, a:a + 1], accum_out=lG[:, a:a + 1])
                last.then_inc(a_eG[c], 1)

            def y_T_high(v, p, h):
                act.wait_ge(p_yT, v + 1)
                av(yTh[:, :, :], t3(B_yT[p]), ACT.Copy).then_inc(a_yTh, 1)

            def q_out_01(v, p, h):
                act.wait_ge(p_q01, v + 1)
                for f in range(2):
                    last = av(qT[:, f, :, :], pairs(B_q01[:, f * 256:(f + 1) * 256]), ACT.Identity, bias=bq[:, h, f:f + 1])
                last.then_inc(a_q01, 2)

            def gate_tanh(v, p, h):
                act.wait_ge(d_gb, v + 1)
                av(gt[:, p, :], gb[:, :], ACT.Tanh, scale=0.5).then_inc(a_gt, 1)

            def k_out_01(v, p, h):
                act.wait_ge(p_k01, v + 1)
                for f in range(2):
                    last = av(kT[:, f, :, :], pairs(B_k01[:, f * 256:(f + 1) * 256]), ACT.Identity, bias=bk[:, h, f:f + 1])
                last.then_inc(a_k01, 2)

            def mask_bias(v, p, h):
                act.wait_ge(s_adj[p], dmas(v, p))
                av(nb[:, :], adj[:, p, :], ACT.Copy, scale=-NEG, bias=NEG).then_inc(a_nb, 1)

            def tanh_h(v, p, h):
                act.wait_ge(d_h, v + 1)
                av(th[:, :], B_h[p][:, 0:D], ACT.Tanh).then_inc(a_th, 1)

            def tanh_T_out(v, p, h):
                act.wait_ge(p_thT, v + 1)
                av(thT[:, :, :], t3(B_thT[p]), ACT.Copy).then_inc(a_thT, 1)

            def gat_probs_T_out(v, p, h, t):
                act.wait_ge(p_ptG[t], v + 1)
                av(ptG[:, 4 * t:4 * t + 4, :], Z3[:, 4 * t:4 * t + 4, :], ACT.Copy).then_inc(a_ptG[t], 1)

            def att_exp(v, p, h, b):
                act.wait_ge(g_bT, v + 1)
                for s in range(3 * b, 3 * b + 3):
                    last = av(pT[:, s, :], S4[:, b, s % 3, :], ACT.Exp, bias=bT[:, s:s + 1], scale=DH ** -0.5,
                              accum_out=lT[:, s:s + 1])
                last.then_inc(a_eT[b], 1)

            def period(do):
                do(1, probs_T_out, 0)
                do(0, x_T_high)
                do(4, weighted_T_out)
                do(-1, x_T_high)
                do(1, probs_T_out, 1)
                do(3, fifth, 1)
                do(3, fifth, 2)
                do(3, fifth, 0)
                do(4, elu_exp)
                do(0, qk_out_2)
                do(1, context_high)
                do(2, mask_not)
                do(3, gat_exp, 4)
                do(3, gat_exp, 5)
                do(2, y_T_high)
                do(0, q_out_01)
                do(3, gate_tanh)
                do(0, k_out_01)
                do(3, gat_exp, 0)
                do(0, mask_bias)
                do(1, mask_not)
                do(2, tanh_h)
                do(3, gat_exp, 1)
                do(3, gat_exp, 3)
                do(2, tanh_T_out)
                do(3, gat_exp, 2)
                do(3, gat_probs_T_out, 2)
                do(3, gat_probs_T_out, 0)
                do(0, att_exp, 1)
                do(3, gat_probs_T_out, 1)
                do(0, att_exp, 0)
                do(2, fifth, 2)
                do(3, weighted_T_out)
                do(2, fifth, 1)
                do(2, fifth, 0)
                do(3, elu_exp)
                do(0, probs_T_out, 0)
                do(-1, mask_bias)
                do(0, probs_T_out, 1)
                do(2, gat_exp, 5)
                do(2, gate_tanh)
                do(0, context_high)
                do(2, gat_exp, 4)
                do(2, gat_exp, 1)
                do(1, y_T_high)
                do(2, gat_exp, 0)
                do(-1, att_exp, 0)
                do(-1, att_exp, 1)
                do(2, gat_exp, 2)
                do(1, tanh_h)
                do(2, gat_exp, 3)
                do(1, tanh_T_out)
                do(2, gat_probs_T_out, 2)
                do(2, gat_probs_T_out, 0)
                do(2, gat_probs_T_out, 1)

            run(act, period)

        @block.vector
        def _(dve):
            vec = nc.vector
            n_set = [0]

            def chained(ins):
                n_set[0] += 1
                ins.then_inc(s_pset, 1)
                dve.wait_ge(s_pset, n_set[0])

            def split_weight(c):
                i, w = c // 6, (Wq, Wk, Wv, Wf, Wg, Wh)[c % 6]
                dve.wait_ge(s_slot[c % 3], 16 * (c // 3 + 1))
                chained(vec.tensor_copy(w[0][:, i, :, :], slot[c % 3]))
                vec.tensor_tensor(w[1][:, i, :, :], slot[c % 3], w[0][:, i, :, :], ALU.subtract).then_inc(s_split[i], 1)

            def second_half(v, p, h):
                if isinstance(v, int) and v == 0:
                    for c in range(6, 12):
                        split_weight(c)

            dve.wait_ge(s_const, 16 * 5)
            chained(vec.tensor_copy(identb[:, :], ident[:, :]))
            chained(vec.tensor_copy(selb[:, :, :, :], bc(selc[:, :, :], 128)))
            chained(vec.memset(mhalf[:, :], -0.5))
            chained(vec.memset(threes[:, :], 3.0))
            chained(vec.memset(eighth[:, :], DH ** -0.5))
            for i in range(2):
                chained(vec.tensor_tensor(sdtmp[:, 0, :, :], sdmask[:, 0, :, :], bc(wsrc[:, i, :], 96), ALU.mult))
                chained(vec.tensor_tensor(sdtmp[:, 1, :, :], sdmask[:, 1, :, :], bc(wdst[:, i, :], 96), ALU.mult))
                chained(vec.tensor_tensor(Wsd[:, i, :, :], sdtmp[:, 0, :, :], sdtmp[:, 1, :, :], ALU.add))
            vec.memset(masked[:, :], -999.0).then_inc(s_setup, 1)
            for c in range(6):
                split_weight(c)
            dve.wait_ge(s_setup, 1)
            dve.wait_ge(s_split[0], 6)

            def gat_divide(v, p, h):
                dve.wait_ge(p_o, v + 1)
                dve.wait_ge(d_rG, v + 1)
                vec.tensor_tensor(o[:, :].rearrange("p (a e) -> p a e", a=GH), B_o[p][:, 0:D].rearrange("p (a e) -> p a e", a=GH),
                                bc(rG[:, :], DG), ALU.mult).then_inc(d_o, 1)

            def below_zero(v, p, h):
                dve.wait_ge(d_o, v + 1)
                vec.tensor_scalar(om[:, :], o[:, :], 0.0, None, ALU.min).then_inc(d_om, 1)

            def leaky(v, p, h, t):
                dve.wait_ge(a_w[t], v + 1)
                vec.tensor_tensor(L[:, 4 * t:4 * t + 4, :], Z3[:, 4 * t:4 * t + 4, :], zw[:, 4 * t:4 * t + 4, :],
                                ALU.max).then_inc(d_L[t], 1)

            def mask(v, p, h, t):
                dve.wait_ge(s_setup, 1)
                dve.wait_ge(a_nota, v + 1)
                dve.wait_ge(d_L[t], v + 1)
                vec.copy_predicated(L[:, 4 * t:4 * t + 4, :], nota[:, p, :].unsqueeze(1).to_broadcast([128, 4, 128]),
                                  masked[:, :].unsqueeze(1).to_broadcast([128, 4, 128])).then_inc(d_pred[t], 1)

            def elu(v, p, h):
                dve.wait_ge(a_e, v + 1)
                vec.scalar_tensor_tensor(oq[:, :], o[:, :], 0.0, oe[:, :], ALU.max, ALU.add).then_inc(d_oq, 1)

            def gat_var_eps(v, p, h):
                dve.wait_ge(d_mv2, v + 1)
                vec.tensor_scalar(ve2[:, :], mv2[:, 1:2], 4.0 * EPS, None, ALU.add).then_inc(d_ve2, 1)

            def gat_max(v, p, h, t):
                dve.wait_ge(d_pred[t], v + 1)
                vec.tensor_reduce(mG[:, 4 * t:4 * t + 4], L[:, 4 * t:4 * t + 4, :], AX.X, ALU.max, negate=True).then_inc(d_mG[t], 1)

            def elu_less_y(v, p, h):
                dve.wait_ge(d_oq, v + 1)
                vec.scalar_tensor_tensor(od[:, :], oq[:, :], 1.0, y[:, p, :], ALU.subtract, ALU.subtract).then_inc(d_od, 1)

            def att_norm(v, p, h):
                dve.wait_ge(g_rs, v + 1)
                if have(v - 2):
                    dve.wait_ge(d_od, v - 1)
                vec.tensor_scalar(y[:, p, :], y0[:, :], mv[:, 0:1], rs[:, :], ALU.subtract, ALU.mult).then_inc(d_y, 1)

            def context_low(v, p, h):
                dve.wait_ge(a_cTh, v + 1)
                vec.tensor_tensor(cTl[:, :, :], t3(B_ctx[p]), cTh[:, :, :], ALU.subtract).then_inc(d_cTl, 1)

            def gat_norm(v, p, h):
                dve.wait_ge(g_rs2, v + 1)
                if have(v - 2):
                    dve.wait_ge(s_st[p], dmas(v - 2, p))
                vec.tensor_scalar(res[:, p, :], os_[:, :], mv2[:, 0:1], rs2[:, :], ALU.subtract, ALU.mult).then_inc(d_res, 1)

            def y_T_low(v, p, h):
                dve.wait_ge(a_yTh, v + 1)
                vec.tensor_tensor(yTl[:, :, :], t3(B_yT[p]), yTh[:, :, :], ALU.subtract).then_inc(d_yTl, 1)

            def h_bias(v, p, h):
                dve.wait_ge(p_h, v + 1)
                vec.tensor_tensor(ha[:, p, :].rearrange("p (a e) -> p a e", a=GH), B_h[p][:, 0:D].rearrange("p (a e) -> p a e", a=GH),
                                bg[:, h, :].unsqueeze(1).to_broadcast([128, GH, DG]), ALU.add).then_inc(d_h, 1)

            def att_sum(v, p, h):
                dve.wait_ge(p_f, v + 1)
                dve.wait_ge(g_xb, v + 1)
                vec.tensor_tensor(y0[:, :], B_f[p][:, 0:D], xb[:, :], ALU.add).then_inc(d_y0, 1)

            def gated_sum(v, p, h):
                dve.wait_ge(g_op, v + 1)
                if have(v - 1):
                    dve.wait_ge(d_res, v)
                vec.scalar_tensor_tensor(os_[:, :], oq[:, :], 4.0, op[:, :], ALU.mult, ALU.add).then_inc(d_os, 1)

            def att_stats(v, p, h):
                dve.wait_ge(d_y0, v + 1)
                vec.bn_stats(st[:, :], y0[:, :]).then_inc(d_st, 1)

            def att_max(v, p, h):
                dve.wait_ge(p_s, v + 1)
                vec.tensor_reduce(mT[:, :].rearrange("p (b j) -> p b j", b=2), S4, AX.X, ALU.max, negate=True).then_inc(d_mT, 1)

            def src_dst_first(v, p, h):
                dve.wait_ge(p_sd, v + 1)
                vec.tensor_copy(sd[:, :], B_sd[p][0:96, 0:128]).then_inc(d_hi, 1)

            def att_mean_var(v, p, h):
                dve.wait_ge(s_setup, 1)
                dve.wait_ge(d_st, v + 1)
                vec.bn_aggr(mv[:, :], st[:, :]).then_inc(d_mv, 1)

            def src_dst_rest(v, p, h):
                dve.wait_ge(d_hi, v + 1)
                vec.tensor_tensor(sr[:, :], B_sd[p][0:96, 0:128], sd[:, :], ALU.subtract).then_inc(d_r1, 1)

            def att_var_eps(v, p, h):
                dve.wait_ge(d_mv, v + 1)
                vec.tensor_scalar(ve[:, :], mv[:, 1:2], EPS, None, ALU.add).then_inc(d_ve, 1)

            def src_dst_second(v, p, h):
                dve.wait_ge(d_r1, v + 1)
                vec.tensor_copy(sd[32:64, :], sr[32:64, :]).then_inc(d_sp1, 1)

            def src_dst_mid(v, p, h):
                vec.tensor_copy(sm[:, :], sr[:, :]).then_inc(d_mid, 1)

            def src_dst_third(v, p, h):
                dve.wait_ge(d_mid, v + 1)
                dve.wait_ge(d_sp1, v + 1)
                vec.tensor_tensor(sd[64:96, :], sr[64:96, :], sm[64:96, :], ALU.subtract).then_inc(d_sd, 1)

            def gat_stats(v, p, h):
                dve.wait_ge(d_os, v + 1)
                vec.bn_stats(st2[:, :], os_[:, :]).then_inc(d_st2, 1)

            def gate_bias(v, p, h):
                dve.wait_ge(p_g, v + 1)
                if have(v - 1):
                    dve.wait_ge(a_gt, v)
                vec.tensor_tensor(gb[:, :], B_g[p][:, 0:D], bh[:, h, :], ALU.add).then_inc(d_gb, 1)

            def att_reciprocal(v, p, h):
                dve.wait_ge(a_eT[0], v + 1)
                dve.wait_ge(a_eT[1], v + 1)
                vec.reciprocal(rT[:, :], lT[:, :]).then_inc(d_rT, 1)

            def gat_reciprocal(v, p, h):
                dve.wait_ge(a_eG[0], v + 1)
                dve.wait_ge(a_eG[1], v + 1)
                dve.wait_ge(a_eG[2], v + 1)
                dve.wait_ge(a_eG[3], v + 1)
                dve.wait_ge(a_eG[4], v + 1)
                dve.wait_ge(a_eG[5], v + 1)
                vec.reciprocal(rG[:, :], lG[:, :]).then_inc(d_rG, 1)

            def gat_mean_var(v, p, h):
                dve.wait_ge(s_setup, 1)
                dve.wait_ge(d_st2, v + 1)
                vec.bn_aggr(mv2[:, :], st2[:, :]).then_inc(d_mv2, 1)

            def v_bias(v, p, h):
                dve.wait_ge(p_v, v + 1)
                vec.tensor_tensor(va[:, :], B_v[p][:, 0:D], bv[:, h, :], ALU.add).then_inc(d_v, 1)

            def x_T_low(v, p, h):
                dve.wait_ge(a_xTh, v + 1)
                vec.tensor_tensor(xTl[:, :, p, :], t3(B_xT[p]), xTh[:, :, p, :], ALU.subtract).then_inc(d_xTl, 1)

            def period(do):
                do(6, gat_divide)
                do(6, below_zero)
                do(5, leaky, 2)
                do(5, mask, 2)
                do(6, elu)
                do(7, gat_var_eps)
                do(5, gat_max, 2)
                do(6, elu_less_y)
                do(4, att_norm)
                do(3, context_low)
                do(5, leaky, 1)
                do(5, leaky, 0)
                do(7, gat_norm)
                do(4, y_T_low)
                do(5, mask, 0)
                do(5, gat_max, 0)
                do(5, mask, 1)
                do(4, h_bias)
                do(5, gat_max, 1)
                do(3, att_sum)
                do(6, gated_sum)
                do(3, att_stats)
                do(2, att_max)
                do(4, src_dst_first)
                do(3, att_mean_var)
                do(4, src_dst_rest)
                do(3, att_var_eps)
                do(4, src_dst_second)
                do(4, src_dst_mid)
                do(4, src_dst_third)
                do(6, gat_stats)
                do(4, gate_bias)
                do(2, att_reciprocal)
                do(5, gat_reciprocal)
                do(6, gat_mean_var)
                do(4, leaky, 2)
                do(6, gat_var_eps)
                do(4, mask, 2)
                do(5, gat_divide)
                do(5, below_zero)
                do(4, leaky, 0)
                do(2, v_bias)
                do(4, gat_max, 2)
                do(5, elu)
                do(4, mask, 0)
                do(5, elu_less_y)
                do(4, gat_max, 0)
                do(3, att_norm)
                do(4, leaky, 1)
                do(2, context_low)
                do(1, att_max)
                do(3, y_T_low)
                do(1, v_bias)
                do(4, mask, 1)
                do(4, gat_max, 1)
                do(2, att_sum)
                do(3, h_bias)
                do(6, gat_norm)
                do(5, gated_sum)
                do(1, att_reciprocal)
                do(3, gate_bias)
                do(5, gat_stats)
                do(4, gat_reciprocal)
                do(2, att_stats)
                do(2, att_mean_var)
                do(3, src_dst_first)
                do(3, src_dst_rest)
                do(3, src_dst_second)
                do(3, src_dst_mid)
                do(3, src_dst_third)
                do(2, att_var_eps)
                do(0, x_T_low)
                do(-1, x_T_low)
                do(5, gat_mean_var)
                do(0, second_half)

            run(dve, period)

        @block.gpsimd
        def _(pool):
            g = nc.gpsimd
            pool.wait_ge(s_setup, 1)

            def att_rstd(v, p, h):
                pool.wait_ge(d_ve, v + 1)
                g.tensor_tensor(rs[:, :], ve[:, :], mhalf[:, :], ALU.pow).then_inc(g_rs, 1)

            def gate_product(v, p, h):
                pool.wait_ge(d_od, v + 1)
                pool.wait_ge(g_ou, v + 1)
                g.tensor_tensor(op[:, :], op[:, :], od[:, :], ALU.mult).then_inc(g_op, 1)

            def gat_rstd(v, p, h):
                pool.wait_ge(d_ve2, v + 1)
                g.tensor_tensor(rs2[:, :], ve2[:, :], mhalf[:, :], ALU.pow).then_inc(g_rs2, 1)

            def att_max_scaled(v, p, h):
                pool.wait_ge(d_mT, v + 1)
                g.tensor_tensor(bT[:, :], mT[:, :], eighth[:, :], ALU.mult).then_inc(g_bT, 1)

            def att_divide(v, p, h, b):
                pool.wait_ge(d_rT, v + 1)
                g.tensor_tensor(pT[:, 3 * b:3 * b + 3, :], pT[:, 3 * b:3 * b + 3, :], bc(rT[:, 3 * b:3 * b + 3], 128),
                                ALU.mult).then_inc(g_pn[b], 1)

            def tanh_less_3(v, p, h):
                pool.wait_ge(a_gt, v + 1)
                if have(v - 1):
                    pool.wait_ge(d_os, v)
                g.tensor_tensor(op[:, :], gt[:, p, :], threes[:, :].to_broadcast([128, D]), ALU.subtract).then_inc(g_ou, 1)

            def residual(v, p, h):
                pool.wait_ge(s_x[p], dmas(v, p))
                if have(v - 1):
                    pool.wait_ge(d_y0, v)
                g.tensor_tensor(xb[:, :], x[:, p, :], bf[:, h, :], ALU.add).then_inc(g_xb, 1)

            def period(do):
                do(2, att_rstd)
                do(4, gate_product)
                do(5, gat_rstd)
                do(0, att_max_scaled)
                do(0, att_divide, 1)
                do(0, att_divide, 0)
                do(3, tanh_less_3)
                do(0, residual)
                do(1, att_rstd)
                do(4, gat_rstd)
                do(3, gate_product)
                do(-1, att_max_scaled)
                do(-1, residual)
                do(-1, att_divide, 0)
                do(-1, att_divide, 1)
                do(2, tanh_less_3)

            run(pool, period)


def kernel(**inputs):
    import numpy as np
    import concourse.bacc as bacc
    from concourse.bass_utils import run_bass_kernel_spmd

    N = NGRAPH
    nc = bacc.Bacc("TRN2", target_bir_lowering=False, num_devices=1)
    arrays = {}
    for name, a in inputs.items():
        a = np.asarray(a)
        if name.endswith("H_w"):
            a = a.T
        if name.endswith("gnn_W"):
            a = a.transpose(1, 0, 2).reshape(384, 384)
        arrays[name] = np.ascontiguousarray(a)
    col = lambda a: a.reshape(3, 128).T
    take = lambda i, n: arrays.pop(f"L{i}_gnn_{n}")
    arrays["cols"] = np.ascontiguousarray(np.stack(
        [np.stack([col(take(*w)) for w in ((2 * i, "bq"), (2 * i, "bk"), (2 * i + 1, "w_src"), (2 * i + 1, "w_dst"))], 1)
         for i in range(2)], 1).reshape(128, -1))
    arrays["rows"] = np.concatenate([take(*w) for i in range(2) for w in (
        (2 * i, "bv"), (2 * i, "bf"), (2 * i + 1, "H_b"), (2 * i + 1, "b"))])
    arrays = {"in_" + n: a for n, a in arrays.items()}
    arrays.update({"in_" + n: a for n, a in _consts().items()})
    aps = {n[3:]: nc.dram_tensor(n, a.shape, mybir.dt.from_np(a.dtype), kind="ExternalInput").ap()
           for n, a in arrays.items()}
    mid = nc.dram_tensor("mid", (N, 128, 384), mybir.dt.float32, kind="Internal").ap()
    out = nc.dram_tensor("out", (N, 128, 384), mybir.dt.float32, kind="ExternalOutput").ap()
    build(nc, N, aps, mid, out)
    r = run_bass_kernel_spmd(nc, [arrays], core_ids=[0])
    return r.results[0]["out"]
```
